# Optimizing a Trainium2 kernel written in Bass

```python
import numpy as np
import jax
import jax.numpy as jnp

def _softmax(x, axis=-1):
    return jax.nn.softmax(x, axis=axis)

def _gelu(x):
    return jax.nn.gelu(x, approximate=True)

def _silu(x):
    return jax.nn.silu(x)

def _sigmoid(x):
    return jax.nn.sigmoid(x)

def _layernorm(x, axis=-1, eps=1e-05):
    m = jnp.mean(x, axis=axis, keepdims=True)
    v = jnp.var(x, axis=axis, keepdims=True)
    return (x - m) / jnp.sqrt(v + eps)

def _scatter_add(tgt, idx, src, axis=0):
    return tgt.at[idx].add(src)

def _segment_sum(src, seg, n):
    return jax.ops.segment_sum(src, seg, n)
kernel_name = 'mk_xattn_ffn_d1_seqx_r4_a3f61a'

def setup_inputs(seed: int=0):
    np.random.seed(seed)
    _w = jnp.asarray

    def _rec_inputs():
        import jax
        import jax.numpy as jnp
        _rk = jax.random.key(seed)
        x = -0.0002928 + 1 * jax.random.normal(jax.random.fold_in(_rk, 1), (2, 1024, 256), jnp.float32)
        _lenS = 1024 - jax.random.randint(jax.random.fold_in(_rk, 7), (2,), 0, max(1, 1024 // 4) + 1, jnp.int32)
        _lenS2 = 64 - jax.random.randint(jax.random.fold_in(_rk, 8), (2,), 0, max(1, 64 // 4) + 1, jnp.int32)
        _ctx_1024P = jax.random.normal(jax.random.fold_in(_rk, 11), (2, 16, 256), jnp.float32)
        _ctx_1024c = jax.random.dirichlet(jax.random.fold_in(_rk, 511), 0.3 * jnp.ones((16,), jnp.float32), (2, 64))
        _ctx_1024t = jnp.einsum('bsk,bkd->bsd', _ctx_1024c, _ctx_1024P)
        _ctx_1024t = _ctx_1024t * jax.lax.rsqrt(jnp.mean(jnp.square(_ctx_1024t)) + 1e-12) * 0.953939
        ctx_1024 = -1.39393e-06 + 0.999914 * (_ctx_1024t + 0.3 * jax.random.normal(jax.random.fold_in(_rk, 611), (2, 64, 256), jnp.float32))
        return (x, ctx_1024)
    x, ctx_1024 = _rec_inputs()

    def _L0_xattn_setup():
        import jax, jax.numpy as jnp
        import numpy as np
        B, S, C = (2, 512, 256)
        H, D = (16, 64)
        key = jax.random.key(seed)
        ks = jax.random.split(key, 8)
        scale_in = 1.0 / np.sqrt(C)
        scale_hd = 1.0 / np.sqrt(H * D)
        return {'inputs_q': jax.random.normal(ks[0], (B, S, C), jnp.float32), 'inputs_kv': jax.random.normal(ks[1], (B, S, C), jnp.float32), 'is_training': 0, 'Wq': jax.random.normal(ks[2], (C, H, D), jnp.float32) * scale_in, 'Wk': jax.random.normal(ks[3], (C, H, D), jnp.float32) * scale_in, 'Wv': jax.random.normal(ks[4], (C, H, D), jnp.float32) * scale_in, 'Wth1': jax.random.normal(ks[5], (H, H), jnp.float32) / np.sqrt(H), 'Wth2': jax.random.normal(ks[6], (H, H), jnp.float32) / np.sqrt(H), 'Wo': jax.random.normal(ks[7], (H, D, C), jnp.float32) * scale_hd}
    _L0_xattn_all = _L0_xattn_setup()
    _L0_xattn_in = {k: v for k, v in _L0_xattn_all.items() if k in ('Wq', 'Wk', 'Wv', 'Wth1', 'Wth2', 'Wo')}
    del _L0_xattn_all

    def _L0_ffn_setup():
        import jax, jax.numpy as jnp
        import numpy as np
        LN_EPS = 1e-05

        def layer_norm(x, g, b):
            mu = jnp.mean(x, axis=-1, keepdims=True)
            var = jnp.var(x, axis=-1, keepdims=True)
            return (x - mu) / jnp.sqrt(var + LN_EPS) * g + b

        def balanced_assignment(scores):
            T, E = scores.shape
            C = T // E
            taken = jnp.zeros((T,), dtype=bool)
            parts = []
            for e in range(E):
                s = jnp.where(taken, -jnp.inf, scores[:, e])
                _, idx = jax.lax.top_k(s, C)
                parts.append(idx)
                taken = taken.at[idx].set(True)
            return jnp.concatenate(parts)
        key = jax.random.key(seed)
        ks = jax.random.split(key, 4)
        B, S, D, F, E = (4, 512, 256, 1024, 8)
        return {'x': jax.random.normal(ks[0], (B, S, D), dtype=jnp.float32), 'centroids': jax.random.normal(ks[1], (E, D), dtype=jnp.float32) * 0.1, 'ln_g': jnp.ones((D,), dtype=jnp.float32), 'ln_b': jnp.zeros((D,), dtype=jnp.float32), 'w1': jax.random.normal(ks[2], (E, D, F), dtype=jnp.float32) * 0.02, 'b1': jnp.zeros((E, F), dtype=jnp.float32), 'w2': jax.random.normal(ks[3], (E, F, D), dtype=jnp.float32) * 0.02, 'b2': jnp.zeros((E, D), dtype=jnp.float32)}
    _L0_ffn_all = _L0_ffn_setup()
    _L0_ffn_in = {k: v for k, v in _L0_ffn_all.items() if k in ('centroids', 'ln_g', 'ln_b', 'w1', 'b1', 'w2', 'b2')}
    del _L0_ffn_all
    return {'x': x, 'ctx_1024': ctx_1024, 'L0_xattn_Wq': _L0_xattn_in['Wq'], 'L0_xattn_Wk': _L0_xattn_in['Wk'], 'L0_xattn_Wv': _L0_xattn_in['Wv'], 'L0_xattn_Wth1': _L0_xattn_in['Wth1'], 'L0_xattn_Wth2': _L0_xattn_in['Wth2'], 'L0_xattn_Wo': _L0_xattn_in['Wo'], 'L0_ffn_centroids': _L0_ffn_in['centroids'], 'L0_ffn_ln_g': _L0_ffn_in['ln_g'], 'L0_ffn_ln_b': _L0_ffn_in['ln_b'], 'L0_ffn_w1': _L0_ffn_in['w1'], 'L0_ffn_b1': _L0_ffn_in['b1'], 'L0_ffn_w2': _L0_ffn_in['w2'], 'L0_ffn_b2': _L0_ffn_in['b2']}

def reference(x, ctx_1024, L0_xattn_Wq, L0_xattn_Wk, L0_xattn_Wv, L0_xattn_Wth1, L0_xattn_Wth2, L0_xattn_Wo, L0_ffn_centroids, L0_ffn_ln_g, L0_ffn_ln_b, L0_ffn_w1, L0_ffn_b1, L0_ffn_w2, L0_ffn_b2):
    import jax
    import jax.numpy as jnp

    def _L0_xattn_ref(inputs_q, inputs_kv, is_training, Wq, Wk, Wv, Wth1, Wth2, Wo):
        import jax, jax.numpy as jnp
        import numpy as np
        B, S, C = (2, 512, 256)
        H, D = (16, 64)
        q = jnp.einsum('bqc,chd->bqhd', inputs_q, Wq) / jnp.sqrt(jnp.asarray(D, inputs_q.dtype))
        k = jnp.einsum('bkc,chd->bkhd', inputs_kv, Wk)
        v = jnp.einsum('bkc,chd->bkhd', inputs_kv, Wv)
        attn = jnp.einsum('bqhd,bkhd->bhqk', q, k)
        attn = jnp.einsum('bhqk,hi->biqk', attn, Wth1)
        attn = jax.nn.softmax(attn, axis=-1)
        attn = jnp.einsum('bhqk,hi->biqk', attn, Wth2)
        out = jnp.einsum('bhqk,bkhd->bqhd', attn, v)
        return jnp.einsum('bqhd,hdc->bqc', out, Wo)

    def _L0_ffn_ref(x, centroids, ln_g, ln_b, w1, b1, w2, b2):
        import jax, jax.numpy as jnp
        import numpy as np
        LN_EPS = 1e-05

        def layer_norm(x, g, b):
            mu = jnp.mean(x, axis=-1, keepdims=True)
            var = jnp.var(x, axis=-1, keepdims=True)
            return (x - mu) / jnp.sqrt(var + LN_EPS) * g + b

        def balanced_assignment(scores):
            T, E = scores.shape
            C = T // E
            taken = jnp.zeros((T,), dtype=bool)
            parts = []
            for e in range(E):
                s = jnp.where(taken, -jnp.inf, scores[:, e])
                _, idx = jax.lax.top_k(s, C)
                parts.append(idx)
                taken = taken.at[idx].set(True)
            return jnp.concatenate(parts)
        D = x.shape[-1]
        feat = x.reshape(-1, D)
        T = feat.shape[0]
        E = centroids.shape[0]
        C = T // E
        norm = layer_norm(feat, ln_g, ln_b)
        scores = jax.lax.stop_gradient(norm @ centroids.T)
        sort_by_expert = balanced_assignment(scores)
        routed = feat[sort_by_expert].reshape(E, C, D)
        h = layer_norm(routed, ln_g, ln_b)
        h = jax.nn.gelu(jnp.einsum('ecd,edf->ecf', h, w1) + b1[:, None, :])
        h = jnp.einsum('ecf,efd->ecd', h, w2) + b2[:, None, :]
        out = routed + h
        inv = jnp.zeros((T,), dtype=jnp.int32).at[sort_by_expert].set(jnp.arange(T, dtype=jnp.int32))
        return out.reshape(T, D)[inv].reshape(x.shape)
    x = x + _L0_xattn_ref(_layernorm(x, axis=-1), ctx_1024, 0, L0_xattn_Wq, L0_xattn_Wk, L0_xattn_Wv, L0_xattn_Wth1, L0_xattn_Wth2, L0_xattn_Wo)
    x = x + _L0_ffn_ref(_layernorm(x, axis=-1), L0_ffn_centroids, L0_ffn_ln_g, L0_ffn_ln_b, L0_ffn_w1, L0_ffn_b1, L0_ffn_w2, L0_ffn_b2)
    return x

_drawn_inputs = setup_inputs


def setup_inputs(seed=0):
    import zlib

    import numpy as np

    out = dict(_drawn_inputs(seed))
    spreads = {'L0_ffn_ln_g': (1.0, 0.2),
     'L0_ffn_ln_b': (0.0, 0.8),
     'L0_ffn_b1': (0.0, 0.466),
     'L0_ffn_b2': (0.0, 0.1)}
    factors = {}
    for name, (base, spread) in spreads.items():
        noise = np.random.default_rng([zlib.crc32(name.encode()), seed]).standard_normal(out[name].shape)
        drawn = base * np.exp(spread * noise) if base else spread * noise
        out[name] = jnp.asarray(drawn.astype(out[name].dtype))
    for name, factor in factors.items():
        out[name] = (out[name] * factor).astype(out[name].dtype)
    return out
```

```python
import concourse.bass as bass
from concourse import mybir
from contextlib import ExitStack

P = 128
B, Q, C = 2, 1024, 256
K, H, D = 64, 16, 64
T = B * Q // P
CC = C // P
HD = H * D
K8 = 8
KG = K // K8
GROUPS = B * KG
COLS = H * K
E, F = 8, 1024
FC = F // P
CAP = B * Q // E
ST = CAP // P
ROUNDS, BITS = 8, 4
TH = 2 ** BITS - 1
LO = 16
EPS = 1e-5
TAKEN = -3.0e38

C_ID, C_TRI, C_I8, C_IOTA, C_TOK, C_SM, C_EX, C_ONE, C_END = 0, 128, 256, 264, 280, 296, 312, 440, 441


def build(nc, x, ctxT, wqT, wk, wv, wo, wth1, wth2T, centT, gb, w1, b1, w2, b2, consts, iconsts, out):
    f32, bf16, i32 = mybir.dt.float32, mybir.dt.bfloat16, mybir.dt.int32
    ALU, ACT, AX = mybir.AluOpType, mybir.ActivationFunctionType, mybir.AxisListType
    ds = bass.ds
    rows_dram = nc.dram_tensor("rows_scratch", (B * Q, 2 * C), f32, kind="Internal").ap()

    with ExitStack() as top:
        def sb(name, shape, dt=f32, ctx=top):
            return ctx.enter_context(nc.sbuf_tensor(name, shape, dt))

        def sem(name):
            return top.enter_context(nc.semaphore(name))

        bank = [top.enter_context(nc.psum_tensor(f"bank{i}", [P, 512], f32)) for i in range(8)]

        cst = sb("cst", [P, C_END])
        ics = sb("ics", [P, ROUNDS * TH], i32)
        tri_b = sb("tri_b", [P, P], bf16)
        ones_b = sb("ones_b", [P, P], bf16)
        cent = sb("cent", [P, CC, E])
        gbs = sb("gbs", [P, 2, CC])
        b1s = sb("b1s", [P, E * FC])
        b2s = sb("b2s", [P, E, C])
        mhalf = sb("mhalf", [P, T])
        ident = cst[:, C_ID:C_ID + P]
        iota = cst[:, C_IOTA:C_IOTA + LO]
        tok = cst[:, C_TOK:C_TOK + T]
        smask = cst[:, C_SM:C_SM + LO]
        expand = cst[0:LO, C_EX:C_EX + P]

        xs = sb("xs", [P, T, C])
        Am = sb("Am", [P, B, CC, COLS])
        Bm = sb("Bm", [P, GROUPS, C])
        bst = sb("bst", [P, T, 6])
        mv1 = sb("mv1", [P, T, 2])
        r1 = sb("r1", [P, T])
        xn = sb("xn", [P, 2, C])
        xnT = sb("xnT", [P, 2, C])
        pr = sb("pr", [P, 2, COLS])
        mxh = sb("mxh", [P, 2, 2, H])
        mx = sb("mx", [P, 2, H])
        sm = sb("sm", [P, 2, H])
        rs = sb("rs", [P, 2, H])
        pT = sb("pT", [P, 2, COLS])
        x1 = sb("x1", [P, 2, C])
        bst2 = sb("bst2", [P, 2, 6])
        mv2 = sb("mv2", [P, 2, 2])
        sc = sb("sc", [P, 2, 8])
        row = sb("row", [P, 2, 2 * C])
        yTs = sb("yTs", [P, 2, C])
        S = sb("S", [P, E, T])

        M = sb("M", [P, T])
        pen = sb("pen", [P, T])
        cmpb = sb("cmpb", [P, TH, T], bf16)
        cntb = sb("cntb", [P, TH], bf16)
        ok = sb("ok", [P, TH])
        jf = sb("jf", [P, 1])
        shi = sb("shi", [P, 1], i32)
        neg = sb("neg", [P, 1], i32)
        jc = sb("jc", [P, 1])
        bits = sb("bits", [P, 2], i32)
        cand = sb("cand", [P, TH], i32)
        GE = sb("GE", [P, 2 * T], bf16)
        INC = sb("INC", [P, 2 * T], bf16)
        EXC = sb("EXC", [P, 2 * T], bf16)
        one_b = sb("one_b", [P, 2 * T], bf16)
        SEL = sb("SEL", [P, 2 * T])
        SLT = sb("SLT", [P, 2 * T])
        slot = sb("slot", [P, T], i32)
        shl = sb("shl", [P, 2, T], i32)
        Loh = sb("Loh", [P, T, LO])
        Hoh = sb("Hoh", [P, T, LO])
        Htk = sb("Htk", [P, T, LO])
        Rt = sb("Rt", [LO, LO])
        Rx = sb("Rx", [P, LO])
        idf = sb("idf", [P, 2, ST])
        idx = sb("idx", [P, 2, ST], i32)

        with ExitStack() as prep:
            ctx_s = sb("ctx_s", [P, CC, B * K], f32, prep)
            wqT_s = sb("wqT_s", [P, HD // P, C], f32, prep)
            wk_s = sb("wk_s", [P, CC, HD], f32, prep)
            wv_s = sb("wv_s", [P, CC, HD], f32, prep)
            wo_s = sb("wo_s", [P, HD // P, C], f32, prep)
            kvT = sb("kvT", [P, 2, HD // P, B * K], f32, prep)
            AB = sb("AB", [P, CC, GROUPS, H, K8], f32, prep)
            ABT = sb("ABT", [P, 2, GROUPS, C], f32, prep)
            wrep = sb("wrep", [P, 2, H], f32, prep)
            mix = sb("mix", [P, 2, H, K8], f32, prep)
        G = sb("G", [P, 2, ST, 2 * C])
        yT = sb("yT", [P, 2, CC, CAP])
        w1s = sb("w1s", [P, 2, CC, F])
        w2s = sb("w2s", [P, 2, FC, C])
        hT = sb("hT", [P, 2, FC, CAP])

        s_in = {n: sem("in_" + n) for n in ("cst", "ctx", "wk", "wv", "wq", "wo", "rep", "small", "x")}
        s_consts, s_mix = sem("consts_made"), sem("mix_made")
        s_fill, s_evA, s_evD = sem("bank_filled"), sem("filled_copied_act"), sem("filled_copied_dve")
        s_bn1, s_mv1, s_ve1, s_r1 = sem("x_stats"), sem("x_mean_var"), sem("x_var_eps"), sem("x_rstd")
        s_xn, s_xT, s_xTs = sem("xn_made"), sem("xn_transposed"), sem("xnT_copied")
        s_lg, s_mx, s_sub, s_exp = sem("logits_made"), sem("max_made"), sem("max_subtracted"), sem("exp_made")
        s_sum, s_rc, s_pn = sem("sum_made"), sem("recip_made"), sem("probs_made")
        s_pT, s_pTs = sem("probs_transposed"), sem("probsT_copied")
        s_pv, s_x1, s_bn2, s_mv2 = sem("attn_made"), sem("x1_made"), sem("x1_stats"), sem("x1_mean_var")
        s_ln, s_yn, s_res = sem("ln_steps"), sem("yn_made"), sem("residual_made")
        s_row = [sem("row_stored_even"), sem("row_stored_odd")]
        s_yT, s_yTs, s_scp, s_sc = sem("yn_transposed"), sem("ynT_copied"), sem("scores_in_psum"), sem("scores_made")
        r_m, r_cmp, r_cnt, r_tot = sem("masked_scores"), sem("compared"), sem("counted"), sem("totals_made")
        r_j, r_jc, r_v, r_neg, r_bits, r_cand = (sem("r_" + n) for n in ("j", "jc", "shifted", "neg", "bits", "cand"))
        r_ge, r_inc, r_exc, r_rank, r_sel = sem("r_ge"), sem("r_inc"), sem("r_exc"), sem("r_rank"), sem("r_sel")
        r_slt, r_slot, r_hl, r_pen1, r_pen = sem("r_slt"), sem("r_slot"), sem("r_hl"), sem("r_pen1"), sem("r_pen")
        r_oh, r_hoh, r_R, r_Rt, r_Rx, r_Rxm = sem("r_oh"), sem("r_hoh"), sem("r_R"), sem("r_Rt"), sem("r_Rx"), sem("r_Rxm")
        r_idf, r_idx = sem("r_idf"), sem("r_idx")
        e_w1 = [sem("w1_even"), sem("w1_odd")]
        e_w2 = [sem("w2_even"), sem("w2_odd")]
        e_g = [sem(f"gathered{i}") for i in range(4)]
        e_gT, e_yT, e_h, e_hs = sem("rows_transposed"), sem("rowsT_copied"), sem("hidden_in_psum"), sem("hidden_made")
        e_o, e_rb, e_fin = sem("expert_out"), sem("residual_bias"), sem("rows_final")
        e_out = [sem(f"rows_scattered{i}") for i in range(4)]

        block = top.enter_context(nc.Block())

        def wait(eng, s, val):
            if isinstance(val, int) and val <= 0:
                return
            eng.wait_ge(s, val)

        def wait_alone(eng, s, val):
            wait(eng, s, val)
            if not isinstance(val, int):
                eng.nop(nofuse=True)

        def steps(eng, first, loop_from, loop_to, last, step):
            for i in range(first, loop_from):
                step(i, i % 2)
            with eng.Fori(loop_from, loop_to - 1, 2) as i:
                step(i, loop_from % 2)
                step(i + 1, 1 - loop_from % 2)
            for i in range(loop_to, last):
                step(i, i % 2)

        def live(t, n=T):
            return not isinstance(t, int) or 0 <= t < n

        def par(t, u, lag):
            return (u - lag) % 2

        A_FIRST, A_LOOP, A_LOOP_END, A_LAST = -1, 7, 15, T + 4
        R_FIRST, R_LOOP, R_LOOP_END, R_LAST = 0, 3, 7, E + 2

        FILLS = 52

        def wait_copied(eng, f):
            wait(eng, s_evA, f // 2 + 1)
            wait(eng, s_evD, (f + 1) // 2)

        def copy_fill(f, do):
            src = bank[f % 8]
            if f < 2:
                do(kvT[:, 0, 4 * f:4 * f + 4, :], src[:].rearrange("p (j n) -> p j n", j=4), D ** -0.5)
            elif f < 4:
                do(kvT[:, 1, 4 * (f - 2):4 * (f - 2) + 4, :], src[:].rearrange("p (j n) -> p j n", j=4), None)
            elif f < 36:
                side, g = (f - 4) // 16, (f - 4) % 16
                if g < 8:
                    cc, odd, m = g // 4, g % 4 // 2, g % 2
                    dst = AB[:, cc, :, :, :].rearrange("p g (m o) k -> p m o g k", o=2)[:, 4 * m:4 * m + 4, odd, :, :]
                    do(dst, src[:].rearrange("p (m g k) -> p m g k", m=4, g=GROUPS), None)
                else:
                    do(ABT[:, side, 2 * (g - 8):2 * (g - 8) + 2, :], src[:].rearrange("p (g c) -> p g c", g=2), None)
            elif f < 44:
                g = f - 36
                do(Am[:, g // 4, g % 4 // 2, (g % 2) * 512:(g % 2 + 1) * 512], src[:], None)
            else:
                g = f - 44
                do(Bm[:, 2 * g:2 * g + 2, :], src[:].rearrange("p (g c) -> p g c", g=2), None)

        @block.sync
        def _(sp):
            sp.dma_start(cst[:], consts).then_inc(s_in["cst"], 16)
            sp.dma_start(ctx_s[:], ctxT.rearrange("(c p) n -> p c n", p=P)).then_inc(s_in["ctx"], 16)
            sp.dma_start(wk_s[:], wk.rearrange("(c p) n -> p c n", p=P)).then_inc(s_in["wk"], 16)
            sp.dma_start(wqT_s[:], wqT.rearrange("(j p) n -> p j n", p=P)).then_inc(s_in["wq"], 16)
            sp.dma_start(wo_s[:], wo.rearrange("(j p) n -> p j n", p=P)).then_inc(s_in["wo"], 16)
            sp.dma_start(ics[:], iconsts).then_inc(s_in["small"], 16)
            sp.dma_start(cent[:], centT.rearrange("(c p) e -> p c e", p=P)).then_inc(s_in["small"], 16)
            sp.dma_start(gbs[:], gb.rearrange("p (a c) -> p a c", a=2)).then_inc(s_in["small"], 16)
            sp.dma_start(b1s[:], b1).then_inc(s_in["small"], 16)
            sp.dma_start(b2s[:], b2.unsqueeze(0).to_broadcast([P, E, C])).then_inc(s_in["small"], 16)

            sp.wait_ge(s_fill, FILLS)
            wait_copied(sp, FILLS - 1)
            for e in range(2):
                sp.dma_start(w1s[:, e], w1[e].rearrange("(c p) f -> p c f", p=P)).then_inc(e_w1[e], 16)
                sp.dma_start(w2s[:, e], w2[e].rearrange("(c p) f -> p c f", p=P)).then_inc(e_w2[e], 16)

            def store_row(s, u):
                t = s - 5
                if live(t):
                    v = par(t, u, 5)
                    wait(sp, s_yn, t + 1)
                    wait(sp, s_res, t + 1)
                    sp.dma_start(rows_dram[ds(t * P, P), :], row[:, v, :]).then_inc(s_row[v], 16)
            steps(sp, A_FIRST, A_LOOP, A_LOOP_END, A_LAST + 1, store_row)

            def load_w(k, u):
                if live(k, E):
                    v = u
                    wait(sp, e_h, FC // 2 * (k - 1))
                    sp.dma_start(w1s[:, v], w1[ds(k, 1)].rearrange("e (c p) f -> p (e c) f", p=P)).then_inc(e_w1[v], 16)
                    wait(sp, e_o, ST * (k - 1))
                    sp.dma_start(w2s[:, v], w2[ds(k, 1)].rearrange("e (c p) f -> p (e c) f", p=P)).then_inc(e_w2[v], 16)
            steps(sp, 2, 2, 8, 8, load_w)

        @block.gpsimd
        def _(pool):
            for o, src in ((0, wth1), (1, wth2T)):
                for k in range(K8):
                    pool.dma_start(wrep[k:P:K8, o, :], src).then_inc(s_in["rep"], 16)
            nc.gpsimd.memset(mhalf[:], -0.5).then_inc(s_consts, 1)
            nc.gpsimd.memset(pen[:], 0.0).then_inc(s_consts, 1)
            nc.gpsimd.memset(one_b[:], 1.0).then_inc(s_consts, 1)
            nc.gpsimd.memset(ones_b[:], 1.0).then_inc(s_consts, 1)
            pool.wait_ge(s_consts, 4)
            pool.wait_ge(s_ve1, 1)
            nc.gpsimd.tensor_tensor(r1[:], r1[:], mhalf[:], ALU.pow).then_inc(s_r1, 1)

            def attn(s, u):
                t = s - 1
                if live(t):
                    v = par(t, u, 1)
                    wait(pool, s_exp, t + 1)
                    wait_alone(pool, s_rc, t + 1)
                    p4 = pr[:, v, :].rearrange("p (g i k) -> p g i k", g=KG, i=H)
                    pool_mul = nc.gpsimd.tensor_tensor(
                        p4, p4, rs[:, v, :].unsqueeze(1).unsqueeze(3).to_broadcast([P, KG, H, K8]), ALU.mult)
                    pool_mul.then_inc(s_pn, 1)
                t = s - 3
                if live(t):
                    v = par(t, u, 3)
                    c = [sc[:, v, n:n + 1] for n in range(8)]
                    m, var = mv2[:, v, 0:1], mv2[:, v, 1:2]
                    wait(pool, s_mv2, t + 1)
                    wait(pool, s_yn, t - 1)
                    wait_alone(pool, s_res, t - 1)
                    n = 9 * t
                    nc.gpsimd.tensor_scalar(c[0], var, 1.0, EPS, ALU.mult, ALU.add).then_inc(s_ln, 1)
                    wait_alone(pool, s_ln, n + 1)
                    nc.gpsimd.tensor_tensor(c[1], c[0], mhalf[:, 0:1], ALU.pow).then_inc(s_ln, 1)
                    wait_alone(pool, s_ln, n + 2)
                    nc.gpsimd.tensor_scalar(c[2], var, c[1], c[1], ALU.mult, ALU.mult).then_inc(s_ln, 1)
                    wait_alone(pool, s_ln, n + 3)
                    nc.gpsimd.tensor_scalar(c[3], c[2], 1.0, EPS, ALU.mult, ALU.add).then_inc(s_ln, 1)
                    wait_alone(pool, s_ln, n + 4)
                    nc.gpsimd.tensor_tensor(c[4], c[3], mhalf[:, 0:1], ALU.pow).then_inc(s_ln, 1)
                    wait_alone(pool, s_ln, n + 5)
                    nc.gpsimd.tensor_scalar(c[5], c[4], c[1], 1.0, ALU.mult, ALU.mult).then_inc(s_ln, 1)
                    wait_alone(pool, s_ln, n + 6)
                    nc.gpsimd.tensor_scalar(c[6], m, c[5], -1.0, ALU.mult, ALU.mult).then_inc(s_ln, 1)
                    nc.gpsimd.tensor_scalar(c[7], m, c[1], -1.0, ALU.mult, ALU.mult).then_inc(s_ln, 1)
                    nc.gpsimd.tensor_scalar(c[3], c[1], 1.0, 1.0, ALU.mult, ALU.add).then_inc(s_ln, 1)
            steps(pool, A_FIRST, A_LOOP, A_LOOP_END, A_LAST, attn)

            for v in range(2):
                pool.wait_ge(s_row[v], 16 * T // 2)
            pool.wait_ge(s_in["small"], 80)

            def gather(e, v, f):
                wait(pool, r_idx, e + 1)
                for a in range(ST):
                    wait_alone(pool, e_out[2 * v + a], 16 * (e // 2))
                for a in range(ST):
                    pool.indirect_dma_start(
                        out=G[:, v, a, :], out_offset=None, in_=rows_dram,
                        in_offset=bass.IndirectOffsetOnAxis(ap=idx[:, v, a:a + 1], axis=0),
                    ).then_inc(e_g[2 * v + a], 16)

            def bias(e, v, h):
                for a in range(ST):
                    wait_alone(pool, e_g[2 * v + a], 16 * h)
                    nc.gpsimd.tensor_tensor(G[:, v, a, C:], G[:, v, a, C:],
                                            b2s[:, ds(e, 1), :].rearrange("p e c -> p (e c)"), ALU.add).then_inc(e_rb, 1)

            def scatter(e, v):
                for a in range(ST):
                    wait_alone(pool, e_fin, ST * e + a + 1)
                    pool.indirect_dma_start(
                        out=out, out_offset=bass.IndirectOffsetOnAxis(ap=idx[:, v, a:a + 1], axis=0),
                        in_=G[:, v, a, C:], in_offset=None).then_inc(e_out[2 * v + a], 16)

            def experts(k, u):
                if live(k - 2, E):
                    scatter(k - 2, u)
                if live(k - 1, E):
                    v = 1 - u
                    gather(k - 1, v, None)
                    bias(k - 1, v, (k + 1) // 2)
            steps(pool, R_FIRST, R_LOOP, R_LOOP_END, R_LAST, experts)
            for i in range(4):
                pool.wait_ge(e_out[i], 16 * E // 2)

        @block.scalar
        def _(act):
            act.dma_start(wv_s[:], wv.rearrange("(c p) n -> p c n", p=P)).then_inc(s_in["wv"], 16)
            act.dma_start(xs[:], x.rearrange("(t p) c -> p t c", p=P)).then_inc(s_in["x"], 16)
            for f in range(0, FILLS, 2):
                def do(dst, src, scale):
                    nc.scalar.activation(dst, src, ACT.Copy, scale=1.0 if scale is None else scale).then_inc(s_evA, 1)
                act.wait_ge(s_fill, f + 1)
                copy_fill(f, do)
            act.wait_ge(s_in["small"], 80)

            def attn(s, u):
                t = s - 1
                if live(t):
                    v = par(t, u, 1)
                    wait(act, s_sub, 2 * t + 2)
                    nc.scalar.activation(pr[:, v, :], pr[:, v, :], ACT.Exp).then_inc(s_exp, 1)
                t = s + 1
                if live(t):
                    v = par(t, u, -1)
                    wait(act, s_xT, t + 1)
                    wait(act, s_lg, t - 1)
                    nc.scalar.activation(xnT[:, v, :], bank[7][:, 0:C], ACT.Copy).then_inc(s_xTs, 1)
                t = s - 2
                if live(t):
                    v = par(t, u, 2)
                    wait(act, s_pv, t - 1)
                    for g in range(2):
                        wait(act, s_pT, 2 * t + g + 1)
                        nc.scalar.activation(pT[:, v, g * 512:(g + 1) * 512], bank[4 + g][:], ACT.Copy).then_inc(s_pTs, 1)
                t = s - 4
                if live(t):
                    v = par(t, u, 4)
                    wait(act, s_yT, t + 1)
                    wait(act, s_scp, t - 1)
                    for c in range(CC):
                        nc.scalar.activation(yTs[:, v, c * P:(c + 1) * P], bank[7][:, c * P:(c + 1) * P], ACT.Identity,
                                             scale=gbs[:, 0, c:c + 1], bias=gbs[:, 1, c:c + 1]).then_inc(s_yTs, 1)
                t = s - 3
                if live(t):
                    v = par(t, u, 3)
                    wait(act, s_ln, 9 * t + 9)
                    wait(act, s_x1, t + 1)
                    wait(act, s_row[v], 16 * (t // 2))
                    wait(act, s_yT, t - 1)
                    nc.scalar.activation(row[:, v, 0:C], x1[:, v, :], ACT.Identity, scale=sc[:, v, 5:6],
                                         bias=sc[:, v, 6:7]).then_inc(s_yn, 1)
            steps(act, A_FIRST, A_LOOP, A_LOOP_END, A_LAST, attn)

            def rows(e, v):
                wait(act, e_gT, e + 1)
                for c in range(CC):
                    nc.scalar.activation(yT[:, v, c, :], bank[0][:, c * CAP:(c + 1) * CAP], ACT.Identity,
                                         scale=gbs[:, 0, c:c + 1], bias=gbs[:, 1, c:c + 1]).then_inc(e_yT, 1)

            def hidden(e, v, g):
                wait(act, e_h, FC // 2 * e + g + 1)
                for h in range(2):
                    f = 2 * g + h
                    nc.scalar.activation(hT[:, v, f, :], bank[1 + g % 3][:, h * CAP:(h + 1) * CAP], ACT.Gelu_apprx_tanh,
                                         bias=b1s[:, ds(e * FC + f, 1)]).then_inc(e_hs, 1)

            def experts(k, u):
                if live(k - 1, E):
                    v = 1 - u
                    wait(act, e_h, FC // 2 * (k - 2))
                    rows(k - 1, v)
                    wait(act, e_o, ST * (k - 2))
                    for g in range(FC // 2):
                        hidden(k - 1, v, g)
            steps(act, R_FIRST, R_LOOP, R_LOOP_END, R_LAST, experts)

        @block.vector
        def _(dve):
            dve.wait_ge(s_in["cst"], 16)
            dve.wait_ge(s_in["rep"], 16 * 2 * K8)
            for o in range(2):
                nc.vector.tensor_tensor(mix[:, o], wrep[:, o, :].unsqueeze(2).to_broadcast([P, H, K8]),
                                        cst[:, C_I8:C_I8 + K8].unsqueeze(1).to_broadcast([P, H, K8]), ALU.mult).then_inc(s_mix, 1)
            nc.vector.tensor_copy(tri_b[:], cst[:, C_TRI:C_TRI + P]).then_inc(s_mix, 1)

            def do(dst, src, scale):
                nc.vector.tensor_copy(dst, src).then_inc(s_evD, 1) if scale is None else \
                    nc.vector.tensor_scalar(dst, src, scale, None, ALU.mult).then_inc(s_evD, 1)
            for f in range(1, FILLS, 2):
                dve.wait_ge(s_fill, f + 1)
                copy_fill(f, do)
                if f == 3:
                    dve.wait_ge(s_in["x"], 16)
                    for t in range(T):
                        nc.vector.bn_stats(bst[:, t, :], xs[:, t, :]).then_inc(s_bn1, 1)
                    for t in range(T):
                        dve.wait_ge(s_bn1, t + 1)
                        nc.vector.bn_aggr(mv1[:, t, :], bst[:, t, :]).then_inc(s_mv1, 1)
                    dve.wait_ge(s_mv1, T)
                    nc.vector.tensor_scalar(r1[:], mv1[:, :, 1], EPS, None, ALU.add).then_inc(s_ve1, 1)
            dve.wait_ge(s_r1, 1)

            def attn(s, u):
                t = s + 1
                if live(t):
                    v = par(t, u, -1)
                    wait(dve, s_xT, t - 1)
                    nc.vector.tensor_scalar(xn[:, v, :], xs[:, ds(t, 1), :].rearrange("p t c -> p (t c)"),
                                            mv1[:, ds(t, 1), 0], r1[:, ds(t, 1)],
                                            ALU.subtract, ALU.mult).then_inc(s_xn, 1)
                t = s - 1
                if live(t):
                    v = par(t, u, 1)
                    wait(dve, s_exp, t + 1)
                    nc.vector.tensor_reduce(sm[:, v, :], pr[:, v, :].rearrange("p (g i k) -> p i g k", g=KG, i=H),
                                            AX.XY, ALU.add).then_inc(s_sum, 1)
                    wait(dve, s_sum, t + 1)
                    wait(dve, s_pn, t - 1)
                    nc.vector.reciprocal(rs[:, v, :], sm[:, v, :]).then_inc(s_rc, 1)
                t = s - 3
                if live(t):
                    v = par(t, u, 3)
                    wait(dve, s_pv, t + 1)
                    wait(dve, s_yn, t - 1)
                    wait(dve, s_res, t - 1)
                    nc.vector.tensor_tensor(x1[:, v, :], bank[6][:, 0:C],
                                            xs[:, ds(t, 1), :].rearrange("p t c -> p (t c)"), ALU.add).then_inc(s_x1, 1)
                    wait(dve, s_x1, t + 1)
                    nc.vector.bn_stats(bst2[:, v, :], x1[:, v, :]).then_inc(s_bn2, 1)
                    wait(dve, s_bn2, t + 1)
                    wait_alone(dve, s_ln, 9 * (t - 1))
                    nc.vector.bn_aggr(mv2[:, v, :], bst2[:, v, :]).then_inc(s_mv2, 1)
                t = s - 4
                if live(t):
                    v = par(t, u, 4)
                    wait(dve, s_ln, 9 * t + 9)
                    wait(dve, s_row[v], 16 * (t // 2))
                    nc.vector.tensor_scalar(row[:, v, C:], x1[:, v, :], sc[:, v, 3:4], sc[:, v, 7:8],
                                            ALU.mult, ALU.add).then_inc(s_res, 1)
                t = s
                if live(t):
                    v = par(t, u, 0)
                    lg = [bank[2 * v][:], bank[2 * v + 1][:]]
                    wait(dve, s_lg, t + 1)
                    for g in range(2):
                        nc.vector.tensor_reduce(mxh[:, v, g, :], lg[g].rearrange("p (g i k) -> p i g k", i=H, k=K8),
                                                AX.XY, ALU.max).then_inc(s_mx, 1)
                    wait(dve, s_mx, 3 * t + 2)
                    nc.vector.tensor_tensor(mx[:, v, :], mxh[:, v, 0, :], mxh[:, v, 1, :], ALU.max).then_inc(s_mx, 1)
                    wait(dve, s_mx, 3 * t + 3)
                    wait(dve, s_pT, 2 * (t - 1))
                    for g in range(2):
                        nc.vector.tensor_tensor(
                            pr[:, v, g * 512:(g + 1) * 512].rearrange("p (g i k) -> p g i k", i=H, k=K8),
                            lg[g].rearrange("p (g i k) -> p g i k", i=H, k=K8),
                            mx[:, v, :].unsqueeze(1).unsqueeze(3).to_broadcast([P, KG // 2, H, K8]),
                            ALU.subtract).then_inc(s_sub, 1)
                t = s - 4
                if live(t):
                    wait(dve, s_scp, t + 1)
                    nc.vector.tensor_copy(S[:, :, ds(t, 1)].rearrange("p e t -> p (e t)"),
                                          bank[7][:, C:C + E]).then_inc(s_sc, 1)
            steps(dve, A_FIRST, A_LOOP, A_LOOP_END, A_LAST, attn)

            dve.wait_ge(s_sc, T)
            dve.wait_ge(s_consts, 4)
            nc.vector.tensor_copy(M[:], S[:, 0, :]).then_inc(r_m, 1)

            def search(k, r):
                n = ROUNDS * k + r
                thr = (ics[:, 0:TH] if r == 0 else cand[:]).bitcast(f32)
                wait(dve, r_m, k + 1)
                if r > 0:
                    wait(dve, r_cand, (ROUNDS - 1) * k + r)
                nc.vector.tensor_tensor(cmpb[:], M[:].unsqueeze(1).to_broadcast([P, TH, T]),
                                        thr.unsqueeze(2).to_broadcast([P, TH, T]), ALU.is_ge).then_inc(r_cmp, 1)
                wait(dve, r_cmp, n + 1)
                wait(dve, r_tot, n)
                with nc.allow_low_precision(reason="counts of at most 16 are exact in bfloat16"):
                    nc.vector.tensor_reduce(cntb[:], cmpb[:], AX.X, ALU.add).then_inc(r_cnt, 1)
                wait(dve, r_tot, n + 1)
                nc.vector.tensor_scalar(ok[:], bank[6][:, 0:TH], float(CAP), 0.0, ALU.is_ge, ALU.add,
                                        accum_out=jf[:]).then_inc(r_j, 1)
                wait(dve, r_j, n + 1)
                a, b = (r + 1) % 2, r % 2
                if r == 0:
                    nc.vector.tensor_scalar(neg[:], jf[:], 8.0, -1.0, ALU.is_lt, ALU.mult).then_inc(r_neg, 1)
                    nc.vector.tensor_scalar(jc[:], jf[:], 8.0, -8.0, ALU.is_ge, ALU.mult).then_inc(r_jc, 1)
                    wait(dve, r_jc, k + 1)
                    nc.vector.tensor_scalar(shi[:], jf[:], jc[:], 2.0 ** 28, ALU.add, ALU.mult).then_inc(r_v, 1)
                    wait(dve, r_neg, k + 1)
                    wait(dve, r_v, n + 1)
                    nc.vector.tensor_tensor(bits[:, b:b + 1], shi[:], neg[:], ALU.bitwise_xor).then_inc(r_bits, 1)
                    wait(dve, r_bits, n + 1)
                    nc.vector.tensor_scalar(cand[:], ics[:, TH:2 * TH], bits[:, b:b + 1], None,
                                            ALU.bitwise_xor).then_inc(r_cand, 1)
                else:
                    nc.vector.tensor_scalar(shi[:], jf[:], 2.0 ** (32 - BITS * (r + 1)), None, ALU.mult).then_inc(r_v, 1)
                    wait(dve, r_v, n + 1)
                    if r < ROUNDS - 1:
                        nc.vector.tensor_scalar(cand[:], ics[:, (r + 1) * TH:(r + 2) * TH], bits[:, a:a + 1], shi[:],
                                                ALU.bitwise_xor, ALU.bitwise_xor).then_inc(r_cand, 1)
                    nc.vector.tensor_tensor(bits[:, b:b + 1], bits[:, a:a + 1], shi[:], ALU.bitwise_xor).then_inc(r_bits, 1)

            def select(k):
                th = bits[:, (ROUNDS - 1) % 2:(ROUNDS - 1) % 2 + 1].bitcast(f32)
                wait(dve, r_bits, ROUNDS * (k + 1))
                wait(dve, r_rank, k)
                nc.vector.tensor_scalar(GE[:, 0:T], M[:], th, None, ALU.is_gt).then_inc(r_ge, 1)
                nc.vector.tensor_scalar(GE[:, T:], M[:], th, None, ALU.is_equal).then_inc(r_ge, 1)
                wait(dve, r_ge, 2 * k + 2)
                nc.vector.tensor_tensor_scan(INC[:], one_b[:], GE[:], 0.0, ALU.mult, ALU.add).then_inc(r_inc, 1)
                wait(dve, r_inc, k + 1)
                nc.vector.tensor_tensor(EXC[:], INC[:], GE[:], ALU.subtract).then_inc(r_exc, 1)
                rank = bank[6][:, 32:32 + 2 * T]
                wait(dve, r_rank, k + 1)
                nc.vector.scalar_tensor_tensor(SEL[:], rank, float(CAP), GE[:], ALU.is_lt, ALU.mult).then_inc(r_sel, 1)
                wait(dve, r_sel, k + 1)
                nc.vector.scalar_tensor_tensor(SLT[:], rank, 1.0, SEL[:], ALU.add, ALU.mult).then_inc(r_slt, 1)
                nc.vector.scalar_tensor_tensor(pen[:], SEL[:, 0:T], TAKEN, pen[:], ALU.mult, ALU.add).then_inc(r_pen1, 1)
                wait(dve, r_pen1, k + 1)
                nc.vector.scalar_tensor_tensor(pen[:], SEL[:, T:], TAKEN, pen[:], ALU.mult, ALU.add).then_inc(r_pen, 1)

            def next_scores(k):
                wait(dve, r_pen, k)
                nc.vector.tensor_tensor(M[:], S[:, ds(k, 1), :].rearrange("p e t -> p (e t)"), pen[:], ALU.add).then_inc(r_m, 1)

            def tokens(k, v):
                wait(dve, r_slt, k + 1)
                nc.vector.scalar_tensor_tensor(slot[:], SLT[:, 0:T], -1.0, SLT[:, T:], ALU.add, ALU.add).then_inc(r_slot, 1)
                wait(dve, r_slot, k + 1)
                nc.vector.tensor_scalar(shl[:, 0, :], slot[:], 15, None, ALU.bitwise_and).then_inc(r_hl, 1)
                nc.vector.tensor_scalar(shl[:, 1, :], slot[:], 4, None, ALU.arith_shift_right).then_inc(r_hl, 1)
                wait(dve, r_hl, 2 * k + 2)
                wait(dve, r_R, k)
                io = iota.unsqueeze(1).to_broadcast([P, T, LO])
                nc.vector.tensor_tensor(Loh[:], io, shl[:, 0, :].unsqueeze(2).to_broadcast([P, T, LO]), ALU.is_equal).then_inc(r_oh, 1)
                nc.vector.tensor_tensor(Hoh[:], io, shl[:, 1, :].unsqueeze(2).to_broadcast([P, T, LO]), ALU.is_equal).then_inc(r_hoh, 1)
                wait(dve, r_hoh, k + 1)
                nc.vector.tensor_tensor(Htk[:], Hoh[:], tok.unsqueeze(2).to_broadcast([P, T, LO]), ALU.mult).then_inc(r_oh, 1)
                wait(dve, r_R, k + 1)
                nc.vector.tensor_copy(Rt[:], bank[7][0:LO, 0:LO]).then_inc(r_Rt, 1)
                wait(dve, r_Rx, k + 1)
                nc.vector.tensor_tensor(Rx[:], bank[7][:, 32:32 + LO], smask, ALU.mult).then_inc(r_Rxm, 1)
                wait(dve, r_Rxm, k + 1)
                nc.vector.tensor_reduce(idf[:, v, :], Rx[:].rearrange("p (a b) -> p a b", a=ST), AX.X, ALU.add).then_inc(r_idf, 1)
                wait(dve, r_idf, k + 1)
                for a in range(ST):
                    wait(dve, e_out[2 * v + a], 16 * (k // 2))
                nc.vector.tensor_copy(idx[:, v, :], idf[:, v, :]).then_inc(r_idx, 1)

            def final(e, v):
                for a in range(ST):
                    wait(dve, e_o, ST * e + a + 1)
                    wait(dve, e_rb, ST * e + a + 1)
                    nc.vector.tensor_tensor(G[:, v, a, C:], bank[4 + a][:, 0:C], G[:, v, a, C:], ALU.add).then_inc(e_fin, 1)

            def experts(k, u):
                if live(k, E) and not (isinstance(k, int) and k == 0):
                    next_scores(k)
                for r in range(ROUNDS):
                    if live(k, E):
                        search(k, r)
                    if r == ROUNDS // 2 - 1 and live(k - 2, E):
                        final(k - 2, u)
                if live(k, E):
                    select(k)
                    tokens(k, u)
            steps(dve, R_FIRST, R_LOOP, R_LOOP_END, R_LAST, experts)

        @block.tensor
        def _(pe):
            def mm(out_, l, r, start, stop):
                return nc.tensor.matmul(out_, l, r, start=start, stop=stop)

            pe.wait_ge(s_in["ctx"], 16)
            f = 0
            for side, (w, name) in enumerate(((wk_s, "wk"), (wv_s, "wv"))):
                pe.wait_ge(s_in[name], 16)
                for g in range(2):
                    for j in range(4):
                        for c in range(CC):
                            last = mm(bank[f][:, j * P:(j + 1) * P], w[:, c, (4 * g + j) * P:(4 * g + j + 1) * P],
                                      ctx_s[:, c, :], c == 0, c == CC - 1)
                    last.then_inc(s_fill, 1)
                    f += 1
            for side, (w, name) in enumerate(((wqT_s, "wq"), (wo_s, "wo"))):
                pe.wait_ge(s_in[name], 16)
                wait_copied(pe, 1 + 2 * side)
                for c in range(CC):
                    if f >= 8:
                        wait_copied(pe, f - 8 + 3)
                    for h in range(H):
                        m, o = h // 2, h % 2
                        q = slice(o * D, (o + 1) * D)
                        last = mm(bank[(f + 2 * o + m // 4) % 8][:, m % 4 * P:(m % 4 + 1) * P],
                                  w[q, m, c * P:(c + 1) * P], kvT[q, side, m, :], True, True)
                    last.then_inc(s_fill, 4)
                    f += 4
                wait_copied(pe, f - 1)
                for g in range(8):
                    wait_copied(pe, f - 8)
                    for h in range(2):
                        for c in range(CC):
                            last = nc.tensor.transpose(bank[f % 8][:, h * C + c * P:h * C + (c + 1) * P],
                                                       AB[:, c, 2 * g + h, :, :].rearrange("p h k -> p (h k)"), ident)
                    last.then_inc(s_fill, 1)
                    f += 1
            pe.wait_ge(s_mix, 3)
            for side in range(2):
                for g in range(8):
                    wait_copied(pe, f - 8)
                    if g == 0 and side == 0:
                        wait_copied(pe, f - 1)
                    if side == 0:
                        for j in range(4):
                            k, c = g // 4 * KG + g % 2 * 4 + j, g % 4 // 2
                            last = mm(bank[f % 8][:, j * P:(j + 1) * P], ABT[:, 0, k, c * P:(c + 1) * P],
                                      mix[:, 0].rearrange("p h k -> p (h k)"), True, True)
                    else:
                        for j in range(2):
                            last = mm(bank[f % 8][:, j * C:(j + 1) * C], mix[:, 1].rearrange("p h k -> p (h k)"),
                                      ABT[:, 1, 2 * g + j, :], True, True)
                    last.then_inc(s_fill, 1)
                    f += 1
            assert f == FILLS
            wait_copied(pe, FILLS - 1)
            pe.wait_ge(s_in["small"], 80)

            def attn(s, u):
                t = s + 1
                if live(t):
                    v = par(t, u, -1)
                    wait(pe, s_xn, t + 1)
                    wait(pe, s_xTs, t)
                    wait(pe, s_sc, s - 4)
                    for c in range(CC):
                        last = nc.tensor.transpose(bank[7][:, c * P:(c + 1) * P], xn[:, v, c * P:(c + 1) * P], ident)
                    last.then_inc(s_xT, 1)
                t = s - 2
                if live(t):
                    v = par(t, u, 2)
                    wait(pe, s_pn, t + 1)
                    for g in range(2):
                        wait(pe, s_pTs, 2 * (t - 1) + g + 1)
                        for j in range(4):
                            q = (4 * g + j) * P
                            last = nc.tensor.transpose(bank[4 + g][:, j * P:(j + 1) * P], pr[:, v, q:q + P], ident)
                        last.then_inc(s_pT, 1)
                t = s - 4
                if live(t):
                    v = par(t, u, 4)
                    wait(pe, s_yn, t + 1)
                    if live(s + 1):
                        wait(pe, s_xTs, s + 2)
                    else:
                        wait(pe, s_sc, t)
                    for c in range(CC):
                        last = nc.tensor.transpose(bank[7][:, c * P:(c + 1) * P], row[:, v, c * P:(c + 1) * P], ident)
                    last.then_inc(s_yT, 1)
                t = s
                if live(t):
                    v = par(t, u, 0)
                    wait(pe, s_xTs, t + 1)
                    wait(pe, s_sub, 2 * (t - 1))
                    for g in range(2):
                        for c in range(CC):
                            last = mm(bank[2 * v + g][:], xnT[:, v, c * P:(c + 1) * P],
                                      Am[:, ds(t // (T // B), 1), c, g * 512:(g + 1) * 512].rearrange("p b n -> p (b n)"),
                                      c == 0, c == CC - 1)
                    last.then_inc(s_lg, 1)
                t = s - 4
                if live(t):
                    v = par(t, u, 4)
                    wait(pe, s_yTs, 2 * t + 2)
                    for c in range(CC):
                        last = mm(bank[7][:, C:C + E], yTs[:, v, c * P:(c + 1) * P], cent[:, c, :], c == 0, c == CC - 1)
                    last.then_inc(s_scp, 1)
                t = s - 2
                if live(t):
                    v = par(t, u, 2)
                    wait(pe, s_x1, t)
                    for g in range(KG):
                        wait(pe, s_pTs, 2 * t + g // 4 + 1)
                        last = mm(bank[6][:, 0:C], pT[:, v, g * P:(g + 1) * P],
                                  Bm[:, ds(t // (T // B) * KG + g, 1), :].rearrange("p g c -> p (g c)"), g == 0, g == KG - 1)
                    last.then_inc(s_pv, 1)
            steps(pe, A_FIRST, A_LOOP, A_LOOP_END, A_LAST, attn)

            pe.wait_ge(s_sc, T)

            def total(k, r):
                n = ROUNDS * k + r
                wait(pe, r_cnt, n + 1)
                wait(pe, r_j, n)
                if r == 0:
                    wait(pe, r_slt, k)
                mm(bank[6][:, 0:TH], ones_b[:], cntb[:], True, True).then_inc(r_tot, 1)

            def ranks(k):
                wait(pe, r_exc, k + 1)
                wait(pe, r_j, ROUNDS * (k + 1))
                mm(bank[6][:, 32:32 + 2 * T], tri_b[:], GE[:], True, False)
                mm(bank[6][:, 32:32 + 2 * T], ones_b[:], EXC[:], False, True).then_inc(r_rank, 1)

            def tokens(k):
                wait(pe, r_oh, 2 * k + 2)
                wait(pe, r_Rxm, k)
                for t in range(T):
                    last = mm(bank[7][0:LO, 0:LO], Loh[:, t, :], Htk[:, t, :], t == 0, t == T - 1)
                last.then_inc(r_R, 1)
                wait(pe, r_Rt, k + 1)
                mm(bank[7][:, 32:32 + LO], expand, Rt[:], True, True).then_inc(r_Rx, 1)

            def rows(e, v, h):
                wait(pe, e_yT, 2 * e)
                for a in range(ST):
                    wait(pe, e_g[2 * v + a], 16 * h)
                    for c in range(CC):
                        last = nc.tensor.transpose(bank[0][:, c * CAP + a * P:c * CAP + (a + 1) * P],
                                                   G[:, v, a, c * P:(c + 1) * P], ident)
                last.then_inc(e_gT, 1)

            def up(e, v, g, h):
                if g == 0:
                    wait(pe, e_w1[v], 16 * h)
                    wait(pe, e_yT, 2 * e + 2)
                b = g % 3
                if g == 3:
                    wait(pe, e_hs, FC * e + 2)
                else:
                    wait(pe, e_hs, FC * (e - 1) + (8 if g == 0 else 2 * g + 2))
                for q in range(2):
                    f = 2 * g + q
                    for c in range(CC):
                        last = mm(bank[1 + b][:, q * CAP:(q + 1) * CAP], w1s[:, v, c, f * P:(f + 1) * P],
                                  yT[:, v, c, :], c == 0, c == CC - 1)
                last.then_inc(e_h, 1)

            def down(e, v, a, q, h):
                if q == 0:
                    wait(pe, e_w2[v], 16 * h)
                    wait(pe, e_fin, ST * e)
                for f in range(q * FC // 2, (q + 1) * FC // 2):
                    if a == 0:
                        wait(pe, e_hs, FC * e + f + 1)
                    last = mm(bank[4 + a][:, 0:C], hT[:, v, f, a * P:(a + 1) * P], w2s[:, v, f, :], f == 0, f == FC - 1)
                if q == 1:
                    last.then_inc(e_o, 1)

            def experts(k, u):
                for r in range(ROUNDS // 2):
                    if live(k, E):
                        total(k, r)
                    if live(k - 2, E):
                        down(k - 2, u, r // 2, r % 2, k // 2)
                if live(k - 1, E):
                    rows(k - 1, 1 - u, (k + 1) // 2)
                for r in range(ROUNDS // 2, ROUNDS):
                    if live(k, E):
                        total(k, r)
                    if live(k - 1, E):
                        up(k - 1, 1 - u, r - ROUNDS // 2, (k + 1) // 2)
                if live(k, E):
                    ranks(k)
                    tokens(k)
            steps(pe, R_FIRST, R_LOOP, R_LOOP_END, R_LAST, experts)


_NAMES = ["x", "ctxT", "wqT", "wk", "wv", "wo", "wth1", "wth2T", "centT", "gb", "w1", "b1", "w2", "b2", "consts", "iconsts"]


def kernel(**inputs):
    import numpy as np
    import concourse.bacc as bacc
    from concourse import mybir as mb
    from concourse.bass_utils import run_bass_kernel_spmd as run

    a = {k: np.asarray(v) for k, v in inputs.items()}
    g, b = a["L0_ffn_ln_g"], a["L0_ffn_ln_b"]
    consts = np.zeros((P, C_END), np.float32)
    p = np.arange(P)
    consts[:, C_ID:C_ID + P] = p[:, None] == p
    consts[:, C_TRI:C_TRI + P] = p[:, None] < p
    consts[:, C_I8:C_I8 + K8] = p[:, None] % K8 == np.arange(K8)
    consts[:, C_IOTA:C_IOTA + LO] = np.arange(LO)
    consts[:, C_TOK:C_TOK + T] = np.arange(T) * P + p[:, None]
    consts[:, C_SM:C_SM + LO] = np.arange(LO) % 8 == p[:, None] // LO
    consts[:LO, C_EX:C_EX + P] = np.arange(LO)[:, None] == p % LO
    ic = np.zeros((ROUNDS, TH), np.int64)
    for r in range(ROUNDS):
        ic[r] = np.arange(1, TH + 1) << (32 - BITS * (r + 1))
    ic[0] = np.where(ic[0] >= 2 ** 31, ic[0] ^ 2 ** 31, ic[0] ^ (2 ** 32 - 1))
    iconsts = np.ascontiguousarray(np.broadcast_to(ic.reshape(1, -1), (P, ROUNDS * TH))).astype(np.uint32).view(np.int32)
    arrays = {
        "x": a["x"].reshape(B * Q, C),
        "ctxT": a["ctx_1024"].reshape(B * K, C).T,
        "wqT": a["L0_xattn_Wq"].transpose(1, 2, 0).reshape(HD, C),
        "wk": a["L0_xattn_Wk"].reshape(C, HD),
        "wv": a["L0_xattn_Wv"].reshape(C, HD),
        "wo": a["L0_xattn_Wo"].reshape(HD, C),
        "wth1": a["L0_xattn_Wth1"],
        "wth2T": a["L0_xattn_Wth2"].T,
        "centT": a["L0_ffn_centroids"].T,
        "gb": np.stack([g.reshape(CC, P).T, b.reshape(CC, P).T], 1).reshape(P, 2 * CC),
        "w1": a["L0_ffn_w1"],
        "b1": a["L0_ffn_b1"].reshape(E * FC, P).T,
        "w2": a["L0_ffn_w2"],
        "b2": a["L0_ffn_b2"],
        "consts": consts,
        "iconsts": iconsts,
    }
    arrays = {k + "_dram": np.ascontiguousarray(v) for k, v in arrays.items()}
    nc = bacc.Bacc("TRN2", target_bir_lowering=False, num_devices=1)
    args = [nc.dram_tensor(n + "_dram", arrays[n + "_dram"].shape, mb.dt.from_np(arrays[n + "_dram"].dtype),
                           kind="ExternalInput").ap() for n in _NAMES]
    out = nc.dram_tensor("out_dram", (B * Q, C), mb.dt.float32, kind="ExternalOutput").ap()
    build(nc, *args, out)
    r = run(nc, [arrays], core_ids=[0])
    return r.results[0]["out_dram"].reshape(B, Q, C)
```

```python
import concourse.bass as bass
from concourse import mybir
from contextlib import ExitStack

P = 128
B, Q, C = 2, 1024, 256
K, H, D = 64, 16, 64
T = B * Q // P
CC = C // P
HD = H * D
K8 = 8
KG = K // K8
GROUPS = B * KG
COLS = H * K
E, F = 8, 1024
FC = F // P
CAP = B * Q // E
ST = CAP // P
ROUNDS, BITS = 8, 4
TH = 2 ** BITS - 1
DIRECT = 3
BASE = 2.0 ** 23
BASE_BITS = 0x4B000000
LO = 16
EPS = 1e-5
TAKEN = -3.0e38

C_ID, C_TRI, C_I8, C_IOTA, C_TOK, C_SM, C_EX, C_W, C_END = 0, 128, 256, 264, 280, 312, 328, 456, 584


def build(nc, x, ctxT, wqT, wk, wv, wo, wth1, wth2T, centT, gb, w1, b1, w2, b2, consts, iconsts, out):
    f32, f32r, bf16, i32 = mybir.dt.float32, mybir.dt.float32r, mybir.dt.bfloat16, mybir.dt.int32
    ALU, ACT, AX = mybir.AluOpType, mybir.ActivationFunctionType, mybir.AxisListType
    ds = bass.ds
    rows_dram = nc.dram_tensor("rows_scratch", (B * Q, 2 * C), f32, kind="Internal").ap()

    with ExitStack() as top:
        def sb(name, shape, dt=f32, ctx=top):
            return ctx.enter_context(nc.sbuf_tensor(name, shape, dt))

        def sem(name):
            return top.enter_context(nc.semaphore(name))

        bank = [top.enter_context(nc.psum_tensor(f"bank{i}", [P, 512], f32)) for i in range(8)]

        cst = sb("cst", [P, C_END])
        ics = sb("ics", [P, ROUNDS * TH + 1], i32)
        tri_b = sb("tri_b", [P, P], bf16)
        ones_b = sb("ones_b", [P, P], bf16)
        cent = sb("cent", [P, CC, E])
        gbs = sb("gbs", [P, 2, CC])
        b1s = sb("b1s", [P, E * FC])
        b2s = sb("b2s", [P, E, C])
        mhalf = sb("mhalf", [P, T])
        ident = cst[:, C_ID:C_ID + P]
        iota = cst[:, C_IOTA:C_IOTA + LO]
        tok = cst[:, C_TOK:C_TOK + 2 * T].rearrange("p (t a) -> p t a", a=2)
        smask = cst[:, C_SM:C_SM + LO]
        expand = cst[0:LO, C_EX:C_EX + P]
        step_w = cst[:, C_W:C_W + ROUNDS * (TH + 1)].rearrange("p (r j) -> p r j", r=ROUNDS)

        xs = sb("xs", [P, T, C])
        Am = sb("Am", [P, 2, B, CC, COLS], f32r)
        Bm = sb("Bm", [P, 2, GROUPS, C], f32r)
        bst = sb("bst", [P, T, 6])
        mv1 = sb("mv1", [P, T, 2])
        r1 = sb("r1", [P, T])
        nmr = sb("nmr", [P, T])



        mxh = sb("mxh", [P, 2, 2, H])
        mx = sb("mx", [P, 2, H])
        sm = sb("sm", [P, 2, H])
        rs = sb("rs", [P, 2, H])


        bst2 = sb("bst2", [P, 2, 6])
        mv2 = sb("mv2", [P, 2, 2])
        sc = sb("sc", [P, 2, 8])


        S = sb("S", [P, E, T])

        M = sb("M", [P, T])
        pen = sb("pen", [P, T])
        Mpre = sb("Mpre", [P, T])
        cmpb = sb("cmpb", [P, TH, T], bf16)
        cntb = sb("cntb", [P, TH + 1], bf16)
        ok = sb("ok", [P, TH + 1])
        acc = sb("acc", [P, 1])
        shi = sb("shi", [P, 1], i32)
        neg = sb("neg", [P, 1], i32)
        bits = sb("bits", [P, 2], i32)
        pre = sb("pre", [P, TH], i32)
        cand = sb("cand", [P, TH], i32)
        GE = sb("GE", [P, 2 * T], bf16)
        INC = sb("INC", [P, 2 * T], bf16)
        one_b = sb("one_b", [P, 2 * T], bf16)
        SEL = sb("SEL", [P, T])
        SLT = sb("SLT", [P, 2 * T])
        slot = sb("slot", [P, T], i32)
        shl = sb("shl", [P, 2, T], i32)
        Loh = sb("Loh", [P, T, LO], bf16)
        Hoh = sb("Hoh", [P, T, LO])
        Htk = sb("Htk", [P, T, 2, LO], bf16)
        Rt = sb("Rt", [LO, 2 * LO])
        Rx = sb("Rx", [P, LO])
        idf = sb("idf", [P, 2, ST])
        idx = sb("idx", [P, 2, ST], i32)

        xn = sb("xn", [P, 2, C])
        xnT = sb("xnT", [P, 2, 2, C], f32r)

        with ExitStack() as prep:
            ctx_s = sb("ctx_s", [P, CC, B * K], f32, prep)
            wqT_s = sb("wqT_s", [P, HD // P, C], f32, prep)
            wo_s = sb("wo_s", [P, HD // P, C], f32, prep)
            kvT = sb("kvT", [P, 2, HD // P, 2, B * K], f32, prep)
            AB = sb("AB", [P, 2, CC, GROUPS, H, K8], f32, prep)
            wrep = sb("wrep", [P, 2, H], f32, prep)
            mix = sb("mix", [P, 2, H, K8], f32, prep)
            with ExitStack() as early:
                wk_s = sb("wk_s", [P, CC, HD], f32, early)
                wv_s = sb("wv_s", [P, CC, HD], f32, early)
            ABT = sb("ABT", [P, 2, GROUPS, C], f32, prep)
        pr = sb("pr", [P, 2, COLS])
        pT = sb("pT", [P, 2, 2, COLS], f32r)
        x1 = sb("x1", [P, 2, C])
        row = sb("row", [P, 2, 2 * C])
        yTs = sb("yTs", [P, 2, C])
        G = sb("G", [P, 2, ST, 2 * C])
        yT = sb("yT", [P, 2, CC, CAP])
        w1s = sb("w1s", [P, 2, CC, F])
        w2s = sb("w2s", [P, 2, FC, C])
        hT = sb("hT", [P, 2, FC, CAP])

        s_in = {n: sem("in_" + n) for n in ("cst", "ctx", "wk", "wv", "wq", "wo", "rep", "small", "x")}
        s_consts, s_zero, s_mix = sem("consts_made"), sem("zeros_made"), sem("mix_made")
        s_fill, s_evA, s_evD = sem("bank_filled"), sem("filled_copied_act"), sem("filled_copied_dve")
        s_bn1, s_mv1, s_ve1, s_r1 = sem("x_stats"), sem("x_mean_var"), sem("x_var_eps"), sem("x_rstd")
        s_nmr, s_xn, s_xT = sem("x_minus_mean_rstd"), sem("xn_made"), sem("xn_transposed")
        s_xTh, s_xTs = sem("xnT_high"), sem("xnT_rest")
        s_lg, s_mx, s_sub, s_exp = sem("logits_made"), sem("max_made"), sem("max_subtracted"), sem("exp_made")
        s_sum, s_rc, s_pn = sem("sum_made"), sem("recip_made"), sem("probs_made")
        s_pT, s_pTh, s_pTs = sem("probs_transposed"), sem("probsT_high"), sem("probsT_rest")
        s_pv, s_x1, s_bn2, s_mv2 = sem("attn_made"), sem("x1_made"), sem("x1_stats"), sem("x1_mean_var")
        s_ln, s_yn, s_res = sem("ln_steps"), sem("yn_made"), sem("residual_made")
        s_row = [sem("row_stored_even"), sem("row_stored_odd")]
        s_yT, s_yTs, s_scp, s_sc = sem("yn_transposed"), sem("ynT_copied"), sem("scores_in_psum"), sem("scores_made")
        r_m, r_cmp, r_cnt, r_tot = sem("masked_scores"), sem("compared"), sem("counted"), sem("totals_made")
        r_j, r_int, r_neg, r_bits, r_pre, r_cand = (sem("r_" + n) for n in ("sum", "sum_int", "neg", "bits", "kept_bits", "cand"))
        r_ge, r_inc, r_rank, r_sel = sem("r_ge"), sem("r_inc"), sem("r_rank"), sem("r_sel")
        r_slt, r_slot, r_hl, r_pen1, r_pen, r_mpre = (sem("r_" + n) for n in ("slt", "slot", "hl", "pen1", "pen", "mpre"))
        r_loh, r_hoh, r_htk = sem("r_loh"), sem("r_hoh"), sem("r_htk")
        r_R, r_Rt, r_Rx, r_Rxm = sem("r_R"), sem("r_Rt"), sem("r_Rx"), sem("r_Rxm")
        r_idf, r_idx = sem("r_idf"), sem("r_idx")
        e_w1 = [sem("w1_even"), sem("w1_odd")]
        e_w2 = [sem("w2_even"), sem("w2_odd")]
        e_g = [sem(f"gathered{i}") for i in range(4)]
        e_gT, e_yT, e_h, e_hs = sem("rows_transposed"), sem("rowsT_copied"), sem("hidden_in_psum"), sem("hidden_made")
        e_o, e_rb, e_fin = sem("expert_out"), sem("residual_bias"), sem("rows_final")
        e_out = [sem(f"rows_scattered{i}") for i in range(4)]

        block = top.enter_context(nc.Block())

        def wait(eng, s, val):
            if isinstance(val, int) and val <= 0:
                return
            eng.wait_ge(s, val)

        def wait_alone(eng, s, val):
            wait(eng, s, val)
            if not isinstance(val, int):
                eng.nop(nofuse=True)

        def steps(eng, first, loop_from, loop_to, last, step):
            for i in range(first, loop_from):
                step(i, i % 2)
            with eng.Fori(loop_from, loop_to - 1, 2) as i:
                step(i, loop_from % 2)
                step(i + 1, 1 - loop_from % 2)
            for i in range(loop_to, last):
                step(i, i % 2)

        def live(t, n=T):
            return not isinstance(t, int) or 0 <= t < n

        def par(t, u, lag):
            return (u - lag) % 2

        A_FIRST, A_LOOP, A_LOOP_END, A_LAST = -2, 7, 13, T + 7
        R_FIRST, R_LOOP, R_LOOP_END, R_LAST = 0, 3, 7, E + 2

        MIXED, FILLS = 36, 52

        def wait_copied(eng, f):
            if f < MIXED:
                wait(eng, s_evA, f // 2 + 1)
                wait(eng, s_evD, (f + 1) // 2)
            else:
                wait(eng, s_evD, MIXED // 2 + f - MIXED + 1)

        def copy_fill(f, copy):
            src = bank[f % 8]
            if f < 4:
                side, g = f // 2, f % 2
                for o in range(2):
                    q = slice(o * D, (o + 1) * D)
                    last = copy(kvT[q, side, 4 * g:4 * g + 4, o, :], src[q].rearrange("p (j n) -> p j n", j=4),
                                1.0 if side else D ** -0.5)
            elif f < 20:
                side, g = (f - 4) // 8, (f - 4) % 8
                cc, h = g // 4, g % 4 * 4
                last = copy(AB[:, side, cc, :, h:h + 4, :].rearrange("p g h k -> p h g k"),
                            src[:].rearrange("p (h g k) -> p h g k", h=4, g=GROUPS), 1.0)
            else:
                side, g = (f - 20) // 8, (f - 20) % 8
                last = copy(ABT[:, side, 2 * g:2 * g + 2, :], src[:].rearrange("p (g c) -> p g c", g=2), 1.0)
            return last

        def mixed(f, part):
            side, g = (f - MIXED) // 8, (f - MIXED) % 8
            if side == 0:
                return Am[:, part, g // 4, g % 4 // 2, (g % 2) * 512:(g % 2 + 1) * 512]
            return Bm[:, part, 2 * g:2 * g + 2, :].rearrange("p g c -> p (g c)")

        @block.sync
        def _(sp):
            sp.dma_start(ctx_s[:], ctxT.rearrange("(c p) n -> p c n", p=P)).then_inc(s_in["ctx"], 16)
            sp.dma_start(wk_s[:], wk.rearrange("(c p) n -> p c n", p=P)).then_inc(s_in["wk"], 16)
            sp.dma_start(wv_s[:], wv.rearrange("(c p) n -> p c n", p=P)).then_inc(s_in["wv"], 16)
            sp.dma_start(wqT_s[:], wqT.rearrange("(j p) n -> p j n", p=P)).then_inc(s_in["wq"], 16)
            sp.dma_start(cst[:], consts).then_inc(s_in["cst"], 16)
            sp.dma_start(wo_s[:], wo.rearrange("(j p) n -> p j n", p=P)).then_inc(s_in["wo"], 16)
            sp.dma_start(xs[:], x.rearrange("(t p) c -> p t c", p=P)).then_inc(s_in["x"], 16)
            sp.dma_start(ics[:], iconsts).then_inc(s_in["small"], 16)
            sp.dma_start(cent[:], centT.rearrange("(c p) e -> p c e", p=P)).then_inc(s_in["small"], 16)
            sp.dma_start(gbs[:], gb.rearrange("p (a c) -> p a c", a=2)).then_inc(s_in["small"], 16)
            sp.dma_start(b1s[:], b1).then_inc(s_in["small"], 16)
            sp.dma_start(b2s[:], b2.unsqueeze(0).to_broadcast([P, E, C])).then_inc(s_in["small"], 16)

            sp.wait_ge(s_fill, FILLS)
            wait_copied(sp, FILLS - 1)
            for e in range(2):
                sp.dma_start(w1s[:, e], w1[e].rearrange("(c p) f -> p c f", p=P)).then_inc(e_w1[e], 16)
                sp.dma_start(w2s[:, e], w2[e].rearrange("(c p) f -> p c f", p=P)).then_inc(e_w2[e], 16)

            def store_row(s, u):
                t = s - 5
                if live(t):
                    v = par(t, u, 5)
                    wait(sp, s_yn, t + 1)
                    wait(sp, s_res, t + 1)
                    sp.dma_start(rows_dram[ds(t * P, P), :], row[:, v, :]).then_inc(s_row[v], 16)
            steps(sp, A_FIRST, A_LOOP, A_LOOP_END, A_LAST + 1, store_row)

            def load_w(k, u):
                if live(k, E):
                    v = u
                    wait(sp, e_h, FC // 2 * (k - 1))
                    sp.dma_start(w1s[:, v], w1[ds(k, 1)].rearrange("e (c p) f -> p (e c) f", p=P)).then_inc(e_w1[v], 16)
                    wait(sp, e_o, ST * (k - 1))
                    sp.dma_start(w2s[:, v], w2[ds(k, 1)].rearrange("e (c p) f -> p (e c) f", p=P)).then_inc(e_w2[v], 16)
            steps(sp, 2, 2, 8, 8, load_w)

        @block.gpsimd
        def _(pool):
            for o in range(2):
                nc.gpsimd.memset(kvT[o * D:(o + 1) * D, :, :, 1 - o, :], 0.0).then_inc(s_zero, 1)
                pool.wait_ge(s_zero, o + 1)
            for o, src in ((0, wth1), (1, wth2T)):
                for k in range(K8):
                    pool.dma_start(wrep[k:P:K8, o, :], src).then_inc(s_in["rep"], 16)
            nc.gpsimd.memset(mhalf[:], -0.5).then_inc(s_consts, 1)
            nc.gpsimd.memset(pen[:], 0.0).then_inc(s_consts, 1)
            nc.gpsimd.memset(one_b[:], 1.0).then_inc(s_consts, 1)
            nc.gpsimd.memset(ones_b[:], 1.0).then_inc(s_consts, 1)
            nc.gpsimd.memset(cntb[:, TH:], float(T)).then_inc(s_consts, 1)
            pool.wait_ge(s_consts, 5)
            pool.wait_ge(s_ve1, 1)
            nc.gpsimd.tensor_tensor(r1[:], r1[:], mhalf[:], ALU.pow).then_inc(s_r1, 1)

            def attn(s, u):
                t = s - 1
                if live(t):
                    v = par(t, u, 1)
                    wait(pool, s_exp, t + 1)
                    wait_alone(pool, s_rc, t + 1)
                    p4 = pr[:, v, :].rearrange("p (g i k) -> p g i k", g=KG, i=H)
                    pool_mul = nc.gpsimd.tensor_tensor(
                        p4, p4, rs[:, v, :].unsqueeze(1).unsqueeze(3).to_broadcast([P, KG, H, K8]), ALU.mult)
                    pool_mul.then_inc(s_pn, 1)
                t = s - 3
                if live(t):
                    v = par(t, u, 3)
                    c = [sc[:, v, n:n + 1] for n in range(8)]
                    m, var = mv2[:, v, 0:1], mv2[:, v, 1:2]
                    wait(pool, s_mv2, t + 1)
                    wait(pool, s_yn, t - 1)
                    wait_alone(pool, s_res, t - 1)
                    n = 9 * t
                    nc.gpsimd.tensor_scalar(c[0], var, 1.0, EPS, ALU.mult, ALU.add).then_inc(s_ln, 1)
                    wait_alone(pool, s_ln, n + 1)
                    nc.gpsimd.tensor_tensor(c[1], c[0], mhalf[:, 0:1], ALU.pow).then_inc(s_ln, 1)
                    wait_alone(pool, s_ln, n + 2)
                    nc.gpsimd.tensor_scalar(c[2], var, c[1], c[1], ALU.mult, ALU.mult).then_inc(s_ln, 1)
                    wait_alone(pool, s_ln, n + 3)
                    nc.gpsimd.tensor_scalar(c[3], c[2], 1.0, EPS, ALU.mult, ALU.add).then_inc(s_ln, 1)
                    wait_alone(pool, s_ln, n + 4)
                    nc.gpsimd.tensor_tensor(c[4], c[3], mhalf[:, 0:1], ALU.pow).then_inc(s_ln, 1)
                    wait_alone(pool, s_ln, n + 5)
                    nc.gpsimd.tensor_scalar(c[5], c[4], c[1], 1.0, ALU.mult, ALU.mult).then_inc(s_ln, 1)
                    wait_alone(pool, s_ln, n + 6)
                    nc.gpsimd.tensor_scalar(c[6], m, c[5], -1.0, ALU.mult, ALU.mult).then_inc(s_ln, 1)
                    nc.gpsimd.tensor_scalar(c[7], m, c[1], -1.0, ALU.mult, ALU.mult).then_inc(s_ln, 1)
                    nc.gpsimd.tensor_scalar(c[3], c[1], 1.0, 1.0, ALU.mult, ALU.add).then_inc(s_ln, 1)
            steps(pool, A_FIRST, A_LOOP, A_LOOP_END, A_LAST, attn)

            for v in range(2):
                pool.wait_ge(s_row[v], 16 * T // 2)
            pool.wait_ge(s_in["small"], 80)

            def token_rows(e):
                wait(pool, r_hoh, e + 1)
                wait_alone(pool, r_R, e)
                nc.gpsimd.tensor_tensor(Htk[:], Hoh[:].unsqueeze(2).to_broadcast([P, T, 2, LO]),
                                        tok.unsqueeze(3).to_broadcast([P, T, 2, LO]), ALU.mult).then_inc(r_htk, 1)

            def gather(e, v):
                wait(pool, r_idx, e + 1)
                for a in range(ST):
                    wait_alone(pool, e_out[2 * v + a], 16 * (e // 2))
                for a in range(ST):
                    pool.indirect_dma_start(
                        out=G[:, v, a, :], out_offset=None, in_=rows_dram,
                        in_offset=bass.IndirectOffsetOnAxis(ap=idx[:, v, a:a + 1], axis=0),
                    ).then_inc(e_g[2 * v + a], 16)

            def bias(e, v, h):
                for a in range(ST):
                    wait_alone(pool, e_g[2 * v + a], 16 * h)
                    nc.gpsimd.tensor_tensor(G[:, v, a, C:], G[:, v, a, C:],
                                            b2s[:, ds(e, 1), :].rearrange("p e c -> p (e c)"), ALU.add).then_inc(e_rb, 1)

            def scatter(e, v):
                for a in range(ST):
                    wait_alone(pool, e_fin, ST * e + a + 1)
                    pool.indirect_dma_start(
                        out=out, out_offset=bass.IndirectOffsetOnAxis(ap=idx[:, v, a:a + 1], axis=0),
                        in_=G[:, v, a, C:], in_offset=None).then_inc(e_out[2 * v + a], 16)

            def experts(k, u):
                if live(k - 1, E):
                    v = 1 - u
                    token_rows(k - 1)
                    gather(k - 1, v)
                    bias(k - 1, v, (k + 1) // 2)
                if live(k - 2, E):
                    scatter(k - 2, u)
            steps(pool, R_FIRST, R_LOOP, R_LOOP_END, R_LAST, experts)
            for i in range(4):
                pool.wait_ge(e_out[i], 16 * E // 2)

        @block.scalar
        def _(act):
            def normalize(t, v):
                nc.scalar.activation(xn[:, v, :], xs[:, ds(t, 1), :].rearrange("p t c -> p (t c)"), ACT.Identity,
                                     scale=r1[:, ds(t, 1)], bias=nmr[:, ds(t, 1)]).then_inc(s_xn, 1)

            for f in range(FILLS):
                if f == MIXED:
                    act.wait_ge(s_nmr, 1)
                    normalize(0, 0)
                    normalize(1, 1)
                if f >= MIXED:
                    act.wait_ge(s_fill, f + 1)
                    nc.scalar.activation(mixed(f, 0), bank[f % 8][:], ACT.Copy).then_inc(s_evA, 1)
                elif f % 2 == 0:
                    act.wait_ge(s_fill, f + 1)
                    copy_fill(f, lambda to, src, scale: nc.scalar.activation(to, src, ACT.Copy, scale=scale)).then_inc(s_evA, 1)
            act.wait_ge(s_in["small"], 80)

            def attn(s, u):
                t = s + 1
                if live(t):
                    v = par(t, u, -1)
                    wait(act, s_xT, t + 1)
                    wait(act, s_lg, t - 1)
                    nc.scalar.activation(xnT[:, 0, v, :], bank[7][:, 0:C], ACT.Copy).then_inc(s_xTh, 1)
                t = s - 1
                if live(t):
                    v = par(t, u, 1)
                    wait(act, s_sub, 2 * t + 2)
                    nc.scalar.activation(pr[:, v, :], pr[:, v, :], ACT.Exp).then_inc(s_exp, 1)
                t = s - 2
                if live(t):
                    v = par(t, u, 2)
                    wait(act, s_pv, t - 1)
                    for g in range(2):
                        wait(act, s_pT, 2 * t + g + 1)
                        nc.scalar.activation(pT[:, 0, v, g * 512:(g + 1) * 512], bank[4 + g][:], ACT.Copy).then_inc(s_pTh, 1)
                t = s + 2
                if live(t) and not (isinstance(s, int) and s < 0):
                    wait(act, s_xT, t - 1)
                    normalize(t, par(t, u, -2))
                t = s - 4
                if live(t):
                    v = par(t, u, 4)
                    wait(act, s_ln, 9 * t + 9)
                    wait(act, s_x1, t + 1)
                    wait(act, s_row[v], 16 * (t // 2))
                    wait(act, s_yT, t - 1)
                    nc.scalar.activation(row[:, v, 0:C], x1[:, v, :], ACT.Identity, scale=sc[:, v, 5:6],
                                         bias=sc[:, v, 6:7]).then_inc(s_yn, 1)
                    nc.scalar.activation(row[:, v, C:], x1[:, v, :], ACT.Identity, scale=sc[:, v, 3:4],
                                         bias=sc[:, v, 7:8]).then_inc(s_res, 1)
                t = s - 5
                if live(t):
                    v = par(t, u, 5)
                    wait(act, s_yT, t + 1)
                    wait(act, s_scp, t - 1)
                    for c in range(CC):
                        nc.scalar.activation(yTs[:, v, c * P:(c + 1) * P], bank[7][:, c * P:(c + 1) * P], ACT.Identity,
                                             scale=gbs[:, 0, c:c + 1], bias=gbs[:, 1, c:c + 1]).then_inc(s_yTs, 1)
            steps(act, A_FIRST, A_LOOP, A_LOOP_END, A_LAST, attn)

            def rows(e, v):
                wait(act, e_gT, e + 1)
                for c in range(CC):
                    nc.scalar.activation(yT[:, v, c, :], bank[0][:, c * CAP:(c + 1) * CAP], ACT.Identity,
                                         scale=gbs[:, 0, c:c + 1], bias=gbs[:, 1, c:c + 1]).then_inc(e_yT, 1)

            def hidden(e, v, g):
                wait(act, e_h, FC // 2 * e + g + 1)
                for h in range(2):
                    f = 2 * g + h
                    nc.scalar.activation(hT[:, v, f, :], bank[1 + g % 3][:, h * CAP:(h + 1) * CAP], ACT.Gelu_apprx_tanh,
                                         bias=b1s[:, ds(e * FC + f, 1)]).then_inc(e_hs, 1)

            def experts(k, u):
                if live(k - 2, E):
                    for g in range(2, FC // 2):
                        hidden(k - 2, u, g)
                if live(k - 1, E):
                    v = 1 - u
                    wait(act, r_R, k)
                    nc.scalar.activation(Rt[:], bank[7][0:LO, 0:2 * LO], ACT.Copy).then_inc(r_Rt, 1)
                    wait(act, e_h, FC // 2 * (k - 2))
                    rows(k - 1, v)
                    wait(act, e_o, ST * (k - 2))
                    for g in range(2):
                        hidden(k - 1, v, g)
            steps(act, R_FIRST, R_LOOP, R_LOOP_END, R_LAST, experts)

        @block.vector
        def _(dve):
            for f in range(FILLS):
                if f >= MIXED:
                    dve.wait_ge(s_evA, MIXED // 2 + f - MIXED + 1)
                    nc.vector.tensor_tensor(mixed(f, 1), bank[f % 8][:], mixed(f, 0).bitcast(f32), ALU.subtract).then_inc(s_evD, 1)
                elif f % 2 == 1:
                    dve.wait_ge(s_fill, f + 1)
                    copy_fill(f, lambda to, src, scale: nc.vector.tensor_scalar(to, src, scale, None, ALU.mult)).then_inc(s_evD, 1)
                if f in (11, 15):
                    dve.wait_ge(s_in["x"], 16)
                    for t in range(T // 2):
                        t += T // 2 if f == 15 else 0
                        nc.vector.bn_stats(bst[:, t, :], xs[:, t, :]).then_inc(s_bn1, 1)
                if f == 15:
                    dve.wait_ge(s_in["cst"], 16)
                    dve.wait_ge(s_in["rep"], 16 * 2 * K8)
                    for o in range(2):
                        nc.vector.tensor_tensor(mix[:, o], wrep[:, o, :].unsqueeze(2).to_broadcast([P, H, K8]),
                                                cst[:, C_I8:C_I8 + K8].unsqueeze(1).to_broadcast([P, H, K8]),
                                                ALU.mult).then_inc(s_mix, 1)
                    nc.vector.tensor_copy(tri_b[:], cst[:, C_TRI:C_TRI + P]).then_inc(s_mix, 1)
                if f == 19:
                    for t in range(T):
                        dve.wait_ge(s_bn1, t + 1)
                        nc.vector.bn_aggr(mv1[:, t, :], bst[:, t, :]).then_inc(s_mv1, 1)
                    dve.wait_ge(s_mv1, T)
                    nc.vector.tensor_scalar(r1[:], mv1[:, :, 1], EPS, None, ALU.add).then_inc(s_ve1, 1)
                if f == 29:
                    dve.wait_ge(s_r1, 1)
                    nc.vector.scalar_tensor_tensor(nmr[:], mv1[:, :, 0], -1.0, r1[:], ALU.mult, ALU.mult).then_inc(s_nmr, 1)

            def attn(s, u):
                t = s - 3
                if live(t):
                    v = par(t, u, 3)
                    wait(dve, s_pv, t + 1)
                    wait(dve, s_yn, t - 1)
                    wait(dve, s_res, t - 1)
                    nc.vector.tensor_tensor(x1[:, v, :], bank[6][:, 0:C],
                                            xs[:, ds(t, 1), :].rearrange("p t c -> p (t c)"), ALU.add).then_inc(s_x1, 1)
                t = s - 7
                if live(t):
                    wait(dve, s_scp, t + 1)
                    if not live(s - 3):
                        wait(dve, s_pv, T)
                    nc.vector.tensor_copy(S[:, :, ds(t, 1)].rearrange("p e t -> p (e t)"),
                                          bank[6][:, C:C + E]).then_inc(s_sc, 1)
                t = s + 1
                if live(t):
                    v = par(t, u, -1)
                    wait(dve, s_xTh, t + 1)
                    nc.vector.tensor_tensor(xnT[:, 1, v, :], bank[7][:, 0:C], xnT[:, 0, v, :].bitcast(f32),
                                            ALU.subtract).then_inc(s_xTs, 1)
                t = s - 3
                if live(t):
                    v = par(t, u, 3)
                    wait(dve, s_x1, t + 1)
                    nc.vector.bn_stats(bst2[:, v, :], x1[:, v, :]).then_inc(s_bn2, 1)
                t = s - 1
                if live(t):
                    v = par(t, u, 1)
                    wait(dve, s_exp, t + 1)
                    nc.vector.tensor_reduce(sm[:, v, :], pr[:, v, :].rearrange("p (g i k) -> p i g k", g=KG, i=H),
                                            AX.XY, ALU.add).then_inc(s_sum, 1)
                t = s - 2
                if live(t):
                    v = par(t, u, 2)
                    q = slice(0, 512)
                    wait(dve, s_pTh, 2 * t + 1)
                    nc.vector.tensor_tensor(pT[:, 1, v, q], bank[4][:], pT[:, 0, v, q].bitcast(f32),
                                            ALU.subtract).then_inc(s_pTs, 1)
                t = s - 1
                if live(t):
                    v = par(t, u, 1)
                    wait(dve, s_sum, t + 1)
                    wait(dve, s_pn, t - 1)
                    nc.vector.reciprocal(rs[:, v, :], sm[:, v, :]).then_inc(s_rc, 1)
                t = s - 3
                if live(t):
                    v = par(t, u, 3)
                    wait(dve, s_bn2, t + 1)
                    wait_alone(dve, s_ln, 9 * (t - 1))
                    nc.vector.bn_aggr(mv2[:, v, :], bst2[:, v, :]).then_inc(s_mv2, 1)
                t = s - 2
                if live(t):
                    v = par(t, u, 2)
                    q = slice(512, 1024)
                    wait(dve, s_pTh, 2 * t + 2)
                    nc.vector.tensor_tensor(pT[:, 1, v, q], bank[5][:], pT[:, 0, v, q].bitcast(f32),
                                            ALU.subtract).then_inc(s_pTs, 1)
                t = s
                if live(t):
                    v = par(t, u, 0)
                    lg = [bank[2 * v][:], bank[2 * v + 1][:]]
                    wait(dve, s_lg, t + 1)
                    for g in range(2):
                        nc.vector.tensor_reduce(mxh[:, v, g, :], lg[g].rearrange("p (g i k) -> p i g k", i=H, k=K8),
                                                AX.XY, ALU.max).then_inc(s_mx, 1)
                    wait(dve, s_mx, 3 * t + 2)
                    nc.vector.tensor_tensor(mx[:, v, :], mxh[:, v, 0, :], mxh[:, v, 1, :], ALU.max).then_inc(s_mx, 1)
                    wait(dve, s_mx, 3 * t + 3)
                    wait(dve, s_pT, 2 * (t - 1))
                    for g in range(2):
                        nc.vector.tensor_tensor(
                            pr[:, v, g * 512:(g + 1) * 512].rearrange("p (g i k) -> p g i k", i=H, k=K8),
                            lg[g].rearrange("p (g i k) -> p g i k", i=H, k=K8),
                            mx[:, v, :].unsqueeze(1).unsqueeze(3).to_broadcast([P, KG // 2, H, K8]),
                            ALU.subtract).then_inc(s_sub, 1)
            steps(dve, A_FIRST, A_LOOP, A_LOOP_END, A_LAST, attn)

            dve.wait_ge(s_sc, T)
            dve.wait_ge(s_consts, 5)
            nc.vector.tensor_copy(M[:], S[:, 0, :]).then_inc(r_m, 1)

            def compare(k, r):
                thr = (ics[:, 0:TH] if r == 0 else cand[:]).bitcast(f32)
                wait(dve, r_m, k + 1)
                if r > 0:
                    wait(dve, r_cand, (ROUNDS - 1) * k + r)
                nc.vector.tensor_tensor(cmpb[:], M[:].unsqueeze(1).to_broadcast([P, TH, T]),
                                        thr.unsqueeze(2).to_broadcast([P, TH, T]), ALU.is_ge).then_inc(r_cmp, 1)

            def count(k, r):
                wait(dve, r_cmp, ROUNDS * k + r + 1)
                with nc.allow_low_precision(reason="counts of at most 16 are exact in bfloat16"):
                    nc.vector.tensor_reduce(cntb[:, 0:TH], cmpb[:], AX.X, ALU.add).then_inc(r_cnt, 1)

            def keep(k, r):
                if r > 0:
                    a = (r + 1) % 2
                    wait(dve, r_bits, ROUNDS * k + r)
                    if r < ROUNDS - 1:
                        nc.vector.tensor_scalar(pre[:], ics[:, (r + 1) * TH:(r + 2) * TH], bits[:, a:a + 1], None,
                                                ALU.bitwise_xor).then_inc(r_pre, 1)
                    else:
                        nc.vector.tensor_tensor(pre[:, 0:1], ics[:, ROUNDS * TH:], bits[:, a:a + 1],
                                                ALU.bitwise_xor).then_inc(r_pre, 1)

            def narrow(k, r):
                n = ROUNDS * k + r
                a, b = (r + 1) % 2, r % 2
                wait(dve, r_tot, n + 1)
                nc.vector.scalar_tensor_tensor(ok[:], bank[6][:, 0:TH + 1], float(CAP), step_w[:, r, :], ALU.is_ge,
                                               ALU.mult, accum_out=acc[:]).then_inc(r_j, 1)
                wait(dve, r_j, n + 1)
                if r < DIRECT:
                    nc.vector.tensor_copy(shi[:], acc[:]).then_inc(r_int, 1)
                    new = shi[:]
                else:
                    new = acc[:].bitcast(i32)
                if r == 0:
                    nc.vector.tensor_scalar(neg[:], ok[:, TH // 2:TH // 2 + 1], 0.0, -1.0, ALU.is_ge, ALU.mult).then_inc(r_neg, 1)
                    wait(dve, r_neg, k + 1)
                if r < DIRECT:
                    wait(dve, r_int, DIRECT * k + r + 1)
                if r == 0:
                    nc.vector.tensor_scalar(cand[:], ics[:, TH:2 * TH], neg[:], new,
                                            ALU.bitwise_xor, ALU.bitwise_xor).then_inc(r_cand, 1)
                    nc.vector.tensor_tensor(bits[:, b:b + 1], new, neg[:], ALU.bitwise_xor).then_inc(r_bits, 1)
                else:
                    wait(dve, r_pre, (ROUNDS - 1) * k + r)
                    if r < ROUNDS - 1:
                        nc.vector.tensor_scalar(cand[:], pre[:], new, None, ALU.bitwise_xor).then_inc(r_cand, 1)
                        nc.vector.tensor_tensor(bits[:, b:b + 1], bits[:, a:a + 1], new, ALU.bitwise_xor).then_inc(r_bits, 1)
                    else:
                        nc.vector.tensor_tensor(bits[:, b:b + 1], pre[:, 0:1], new, ALU.bitwise_xor).then_inc(r_bits, 1)

            def select(k):
                th = bits[:, (ROUNDS - 1) % 2:(ROUNDS - 1) % 2 + 1].bitcast(f32)
                wait(dve, r_bits, ROUNDS * (k + 1))
                nc.vector.tensor_scalar(GE[:, 0:T], M[:], th, None, ALU.is_gt).then_inc(r_ge, 1)
                nc.vector.tensor_scalar(GE[:, T:], M[:], th, None, ALU.is_equal).then_inc(r_ge, 1)
                wait(dve, r_ge, 2 * k + 2)
                nc.vector.tensor_tensor_scan(INC[:], one_b[:], GE[:], 0.0, ALU.mult, ALU.add).then_inc(r_inc, 1)
                wait(dve, r_pen, k)
                nc.vector.scalar_tensor_tensor(pen[:], GE[:, 0:T], TAKEN, pen[:], ALU.mult, ALU.add).then_inc(r_pen1, 1)
                wait(dve, r_pen1, k + 1)
                if live(k + 1, E):
                    nc.vector.tensor_tensor(Mpre[:], S[:, ds(k + 1, 1), :].rearrange("p e t -> p (e t)"), pen[:],
                                            ALU.add).then_inc(r_mpre, 1)
                rank = bank[6][:, 32:32 + 2 * T]
                wait(dve, r_rank, k + 1)
                nc.vector.scalar_tensor_tensor(SEL[:], rank[:, T:], float(CAP), GE[:, T:], ALU.is_lt, ALU.mult).then_inc(r_sel, 1)
                nc.vector.scalar_tensor_tensor(SLT[:, 0:T], rank[:, 0:T], 1.0, GE[:, 0:T], ALU.add, ALU.mult).then_inc(r_slt, 1)
                wait(dve, r_sel, k + 1)
                if live(k + 1, E):
                    wait(dve, r_mpre, k + 1)
                    nc.vector.scalar_tensor_tensor(M[:], SEL[:], TAKEN, Mpre[:], ALU.mult, ALU.add).then_inc(r_m, 1)
                nc.vector.scalar_tensor_tensor(SLT[:, T:], rank[:, T:], 1.0, SEL[:], ALU.add, ALU.mult).then_inc(r_slt, 1)

            def slots(k):
                wait(dve, r_slt, 2 * k + 2)
                nc.vector.scalar_tensor_tensor(slot[:], SLT[:, 0:T], -1.0, SLT[:, T:], ALU.add, ALU.add).then_inc(r_slot, 1)
                nc.vector.scalar_tensor_tensor(pen[:], SEL[:], TAKEN, pen[:], ALU.mult, ALU.add).then_inc(r_pen, 1)

            def halves(k):
                wait(dve, r_slot, k + 1)
                nc.vector.tensor_scalar(shl[:, 1, :], slot[:], 4, None, ALU.arith_shift_right).then_inc(r_hl, 1)
                nc.vector.tensor_scalar(shl[:, 0, :], slot[:], 15, None, ALU.bitwise_and).then_inc(r_hl, 1)

            def one_hot(k, half, to, s):
                wait(dve, r_R, k)
                wait(dve, r_hl, 2 * k + 2)
                nc.vector.tensor_tensor(to[:], iota.unsqueeze(1).to_broadcast([P, T, LO]),
                                        shl[:, half, :].unsqueeze(2).to_broadcast([P, T, LO]), ALU.is_equal).then_inc(s, 1)

            def indices(k, v):
                wait(dve, r_Rx, k + 1)
                nc.vector.tensor_tensor(Rx[:], bank[7][:, 32:32 + LO], smask, ALU.mult).then_inc(r_Rxm, 1)
                wait(dve, r_Rxm, k + 1)
                nc.vector.tensor_reduce(idf[:, v, :], Rx[:].rearrange("p (a b) -> p a b", a=ST), AX.X, ALU.add).then_inc(r_idf, 1)
                for a in range(ST):
                    wait(dve, e_out[2 * v + a], 16 * (k // 2))
                wait(dve, r_idf, k + 1)
                nc.vector.tensor_copy(idx[:, v, :], idf[:, v, :]).then_inc(r_idx, 1)

            def final(e, v, a):
                wait(dve, e_o, ST * e + a + 1)
                wait(dve, e_rb, ST * e + a + 1)
                nc.vector.tensor_tensor(G[:, v, a, C:], bank[4 + a][:, 0:C], G[:, v, a, C:], ALU.add).then_inc(e_fin, 1)

            def experts(k, u):
                for r in range(ROUNDS):
                    if live(k, E):
                        compare(k, r)
                        keep(k, r)
                    if r == 0 and live(k - 1, E):
                        slots(k - 1)
                    if live(k, E):
                        count(k, r)
                    if r == 0 and live(k - 1, E):
                        halves(k - 1)
                        one_hot(k - 1, 1, Hoh, r_hoh)
                    if r == 1 and live(k - 1, E):
                        one_hot(k - 1, 0, Loh, r_loh)
                    if r == 3 and live(k - 1, E):
                        indices(k - 1, 1 - u)
                    if r in (4, 6) and live(k - 2, E):
                        final(k - 2, u, (r - 4) // 2)
                    if live(k, E):
                        narrow(k, r)
                if live(k, E):
                    select(k)
            steps(dve, R_FIRST, R_LOOP, R_LOOP_END, R_LAST, experts)

        @block.tensor
        def _(pe):
            def mm(out_, l, r, start, stop):
                return nc.tensor.matmul(out_, l, r, start=start, stop=stop)

            def mm3(out_, l, r, start, stop):
                mm(out_, l(0), r(0), start, False)
                mm(out_, l(0), r(1), False, False)
                return mm(out_, l(1), r(0), False, stop)

            pe.wait_ge(s_in["ctx"], 16)
            f = 0
            for w, name in ((wk_s, "wk"), (wv_s, "wv")):
                pe.wait_ge(s_in[name], 16)
                for g in range(2):
                    for j in range(4):
                        for c in range(CC):
                            last = mm(bank[f][:, j * P:(j + 1) * P], w[:, c, (4 * g + j) * P:(4 * g + j + 1) * P],
                                      ctx_s[:, c, :], c == 0, c == CC - 1)
                    last.then_inc(s_fill, 1)
                    f += 1
            pe.wait_ge(s_zero, 2)
            for side, (w, name) in enumerate(((wqT_s, "wq"), (wo_s, "wo"))):
                pe.wait_ge(s_in[name], 16)
                wait_copied(pe, 1 + 2 * side)
                for c in range(CC):
                    if f >= 8:
                        wait_copied(pe, f - 5)
                    for m in range(HD // P):
                        last = mm(bank[(f + m // 2) % 8][:, m % 2 * 2 * P:(m % 2 + 1) * 2 * P],
                                  w[:, m, c * P:(c + 1) * P], kvT[:, side, m].rearrange("p o n -> p (o n)"), True, True)
                    last.then_inc(s_fill, 4)
                    f += 4
            pe.wait_ge(s_in["cst"], 16)
            for side in range(2):
                for g in range(8):
                    wait_copied(pe, max(f - 8, 11 + 8 * side))
                    for h in range(2):
                        for c in range(CC):
                            last = nc.tensor.transpose(bank[f % 8][:, h * C + c * P:h * C + (c + 1) * P],
                                                       AB[:, side, c, 2 * g + h, :, :].rearrange("p h k -> p (h k)"), ident)
                    last.then_inc(s_fill, 1)
                    f += 1
            pe.wait_ge(s_mix, 3)
            for side in range(2):
                mix_s = mix[:, side].rearrange("p h k -> p (h k)")
                for g in range(8):
                    wait_copied(pe, max(f - 8, 27 + 8 * side))
                    if side == 0:
                        for j in range(4):
                            k, c = g // 4 * KG + g % 2 * 4 + j, g % 4 // 2
                            last = mm(bank[f % 8][:, j * P:(j + 1) * P], ABT[:, 0, k, c * P:(c + 1) * P], mix_s, True, True)
                    else:
                        for j in range(2):
                            last = mm(bank[f % 8][:, j * C:(j + 1) * C], mix_s, ABT[:, 1, 2 * g + j, :], True, True)
                    last.then_inc(s_fill, 1)
                    f += 1
            assert f == FILLS
            wait_copied(pe, FILLS - 1)
            pe.wait_ge(s_in["small"], 80)

            def attn(s, u):
                t = s + 1
                if live(t):
                    v = par(t, u, -1)
                    wait(pe, s_xn, t + 1)
                    wait(pe, s_xTs, t)
                    wait(pe, s_yTs, 2 * (s - 5))
                    for c in range(CC):
                        last = nc.tensor.transpose(bank[7][:, c * P:(c + 1) * P], xn[:, v, c * P:(c + 1) * P], ident)
                    last.then_inc(s_xT, 1)
                t = s - 2
                if live(t):
                    v = par(t, u, 2)
                    wait(pe, s_pn, t + 1)
                    for g in range(2):
                        wait(pe, s_pTs, 2 * (t - 1) + g + 1)
                        for j in range(4):
                            q = (4 * g + j) * P
                            last = nc.tensor.transpose(bank[4 + g][:, j * P:(j + 1) * P], pr[:, v, q:q + P], ident)
                        last.then_inc(s_pT, 1)
                t = s
                if live(t):
                    v = par(t, u, 0)
                    wait(pe, s_xTs, t + 1)
                    wait(pe, s_sub, 2 * (t - 1))
                    for g in range(2):
                        for c in range(CC):
                            last = mm3(bank[2 * v + g][:], lambda i: xnT[:, i, v, c * P:(c + 1) * P],
                                       lambda i: Am[:, i, ds(t // (T // B), 1), c, g * 512:(g + 1) * 512].rearrange(
                                           "p b n -> p (b n)"), c == 0, c == CC - 1)
                    last.then_inc(s_lg, 1)
                t = s - 5
                if live(t):
                    v = par(t, u, 5)
                    wait(pe, s_yn, t + 1)
                    if live(s + 1):
                        wait(pe, s_xTs, s + 2)
                    else:
                        wait(pe, s_yTs, 2 * t)
                    for c in range(CC):
                        last = nc.tensor.transpose(bank[7][:, c * P:(c + 1) * P], row[:, v, c * P:(c + 1) * P], ident)
                    last.then_inc(s_yT, 1)
                t = s - 6
                if live(t):
                    v = par(t, u, 6)
                    wait(pe, s_yTs, 2 * t + 2)
                    wait(pe, s_x1, min(s - 2, T) if isinstance(s, int) else s - 2)
                    wait(pe, s_sc, t)
                    for c in range(CC):
                        last = mm(bank[6][:, C:C + E], yTs[:, v, c * P:(c + 1) * P], cent[:, c, :], c == 0, c == CC - 1)
                    last.then_inc(s_scp, 1)
                t = s - 2
                if live(t):
                    v = par(t, u, 2)
                    wait(pe, s_x1, t)
                    for g in range(KG):
                        wait(pe, s_pTs, 2 * t + g // 4 + 1)
                        last = mm3(bank[6][:, 0:C], lambda i: pT[:, i, v, g * P:(g + 1) * P],
                                   lambda i: Bm[:, i, ds(t // (T // B) * KG + g, 1), :].rearrange("p g c -> p (g c)"),
                                   g == 0, g == KG - 1)
                    last.then_inc(s_pv, 1)
            steps(pe, A_FIRST, A_LOOP, A_LOOP_END, A_LAST, attn)

            pe.wait_ge(s_sc, T)

            def total(k, r):
                wait(pe, r_cnt, ROUNDS * k + r + 1)
                wait(pe, r_j, ROUNDS * k + r)
                if r == 0:
                    wait(pe, r_slt, 2 * k)
                mm(bank[6][:, 0:TH + 1], ones_b[:], cntb[:], True, True).then_inc(r_tot, 1)

            def ranks(k):
                wait(pe, r_ge, 2 * k + 2)
                wait(pe, r_j, ROUNDS * (k + 1))
                mm(bank[6][:, 32:32 + 2 * T], tri_b[:], GE[:], True, False)
                wait(pe, r_inc, k + 1)
                mm(bank[6][:, 32:32 + 2 * T], ones_b[:], INC[:], False, True).then_inc(r_rank, 1)

            def tokens(k):
                wait(pe, r_htk, k + 1)
                wait(pe, r_loh, k + 1)
                wait(pe, r_Rxm, k)
                for t in range(T):
                    last = mm(bank[7][0:LO, 0:2 * LO], Loh[:, t, :], Htk[:, t].rearrange("p a h -> p (a h)"), t == 0, t == T - 1)
                last.then_inc(r_R, 1)

            def spread(k):
                wait(pe, r_Rt, k + 1)
                mm(bank[7][:, 32:32 + LO], expand, Rt[:, 0:LO], True, False)
                mm(bank[7][:, 32:32 + LO], expand, Rt[:, LO:], False, True).then_inc(r_Rx, 1)

            def rows(e, v, h):
                wait(pe, e_yT, 2 * e)
                for a in range(ST):
                    wait(pe, e_g[2 * v + a], 16 * h)
                    for c in range(CC):
                        last = nc.tensor.transpose(bank[0][:, c * CAP + a * P:c * CAP + (a + 1) * P],
                                                   G[:, v, a, c * P:(c + 1) * P], ident)
                last.then_inc(e_gT, 1)

            def up(e, v, f, h):
                if f == 0:
                    wait(pe, e_w1[v], 16 * h)
                    wait(pe, e_yT, 2 * e + 2)
                g, q = f // 2, f % 2
                if q == 0:
                    if g == 3:
                        wait(pe, e_hs, FC * e + 2)
                    else:
                        wait(pe, e_hs, FC * (e - 1) + (8 if g == 0 else 2 * g + 2))
                for c in range(CC):
                    last = mm(bank[1 + g % 3][:, q * CAP:(q + 1) * CAP], w1s[:, v, c, f * P:(f + 1) * P],
                              yT[:, v, c, :], c == 0, c == CC - 1)
                if q == 1:
                    last.then_inc(e_h, 1)

            def down(e, v, n, h):
                a, f = n // FC, n % FC
                if n == 0:
                    wait(pe, e_w2[v], 16 * h)
                    wait(pe, e_fin, ST * (e - 1) + 1)
                if n == FC:
                    wait(pe, e_fin, ST * e)
                if a == 0:
                    wait(pe, e_hs, FC * e + f + 1)
                last = mm(bank[4 + a][:, 0:C], hT[:, v, f, a * P:(a + 1) * P], w2s[:, v, f, :], f == 0, f == FC - 1)
                if f == FC - 1:
                    last.then_inc(e_o, 1)

            UP_TAIL, DOWN, UP_HEAD = {0: (6, 8)}, {1: (0, 2), 2: (2, 5), 3: (5, 9), 4: (9, 12), 5: (12, 14)}, {6: (0, 2), 7: (2, 4)}

            def experts(k, u):
                if live(k - 2, E):
                    for f in range(4, 6):
                        up(k - 2, u, f, k // 2)
                for r in range(ROUNDS):
                    if live(k, E):
                        total(k, r)
                    if live(k - 1, E):
                        if r == 2:
                            spread(k - 1)
                    if live(k - 2, E):
                        for f in range(*UP_TAIL.get(r, (0, 0))):
                            up(k - 2, u, f, k // 2)
                        for n in range(*DOWN.get(r, (0, 0))):
                            down(k - 2, u, n, k // 2)
                    if r == 5 and live(k - 1, E):
                        rows(k - 1, 1 - u, (k + 1) // 2)
                    if r == 5 and live(k - 2, E):
                        for n in range(DOWN[5][1], 2 * FC):
                            down(k - 2, u, n, k // 2)
                    if r == 1 and live(k - 1, E):
                        tokens(k - 1)
                    if live(k - 1, E):
                        for f in range(*UP_HEAD.get(r, (0, 0))):
                            up(k - 1, 1 - u, f, (k + 1) // 2)
                if live(k, E):
                    ranks(k)
            steps(pe, R_FIRST, R_LOOP, R_LOOP_END, R_LAST, experts)


_NAMES = ["x", "ctxT", "wqT", "wk", "wv", "wo", "wth1", "wth2T", "centT", "gb", "w1", "b1", "w2", "b2", "consts", "iconsts"]


def kernel(**inputs):
    import numpy as np
    import concourse.bacc as bacc
    from concourse import mybir as mb
    from concourse.bass_utils import run_bass_kernel_spmd as run

    a = {k: np.asarray(v) for k, v in inputs.items()}
    g, b = a["L0_ffn_ln_g"], a["L0_ffn_ln_b"]
    consts = np.zeros((P, C_END), np.float32)
    p = np.arange(P)
    consts[:, C_ID:C_ID + P] = p[:, None] == p
    consts[:, C_TRI:C_TRI + P] = (p[:, None] < p) - 1.0
    consts[:, C_I8:C_I8 + K8] = p[:, None] % K8 == np.arange(K8)
    consts[:, C_IOTA:C_IOTA + LO] = np.arange(LO)
    consts[:, C_TOK:C_TOK + 2 * T:2] = np.arange(T) * P
    consts[:, C_TOK + 1:C_TOK + 2 * T:2] = p[:, None]
    consts[:, C_SM:C_SM + LO] = np.arange(LO) % 8 == p[:, None] // LO
    for r in range(ROUNDS):
        w = consts[:, C_W + r * (TH + 1):C_W + (r + 1) * (TH + 1)]
        w[:, :TH] = 2.0 ** (32 - BITS * (r + 1))
        w[:, TH] = BASE if r >= DIRECT else 0.0
    consts[:, C_W + 7] *= -7.0
    consts[:LO, C_EX:C_EX + P] = np.arange(LO)[:, None] == p % LO
    ic = np.zeros((ROUNDS, TH), np.int64)
    for r in range(ROUNDS):
        ic[r] = np.arange(1, TH + 1) << (32 - BITS * (r + 1))
        if r > DIRECT and (r - DIRECT) % 2:
            ic[r] ^= BASE_BITS
    ic[0] = np.where(ic[0] >= 2 ** 31, ic[0] ^ 2 ** 31, ic[0] ^ (2 ** 32 - 1))
    ic = np.concatenate([ic.reshape(-1), [BASE_BITS]])
    iconsts = np.ascontiguousarray(np.broadcast_to(ic.reshape(1, -1), (P, ROUNDS * TH + 1))).astype(np.uint32).view(np.int32)
    arrays = {
        "x": a["x"].reshape(B * Q, C),
        "ctxT": a["ctx_1024"].reshape(B * K, C).T,
        "wqT": a["L0_xattn_Wq"].transpose(1, 2, 0).reshape(HD, C),
        "wk": a["L0_xattn_Wk"].reshape(C, HD),
        "wv": a["L0_xattn_Wv"].reshape(C, HD),
        "wo": a["L0_xattn_Wo"].reshape(HD, C),
        "wth1": a["L0_xattn_Wth1"],
        "wth2T": a["L0_xattn_Wth2"].T,
        "centT": a["L0_ffn_centroids"].T,
        "gb": np.stack([g.reshape(CC, P).T, b.reshape(CC, P).T], 1).reshape(P, 2 * CC),
        "w1": a["L0_ffn_w1"],
        "b1": a["L0_ffn_b1"].reshape(E * FC, P).T,
        "w2": a["L0_ffn_w2"],
        "b2": a["L0_ffn_b2"],
        "consts": consts,
        "iconsts": iconsts,
    }
    arrays = {k + "_dram": np.ascontiguousarray(v) for k, v in arrays.items()}
    nc = bacc.Bacc("TRN2", target_bir_lowering=False, num_devices=1)
    args = [nc.dram_tensor(n + "_dram", arrays[n + "_dram"].shape, mb.dt.from_np(arrays[n + "_dram"].dtype),
                           kind="ExternalInput").ap() for n in _NAMES]
    out = nc.dram_tensor("out_dram", (B * Q, C), mb.dt.float32, kind="ExternalOutput").ap()
    build(nc, *args, out)
    r = run(nc, [arrays], core_ids=[0])
    return r.results[0]["out_dram"].reshape(B, Q, C)
```

```python
import concourse.bass as bass
from concourse import mybir
from contextlib import ExitStack

P = 128
B, Q, C = 2, 1024, 256
K, H, D = 64, 16, 64
T = B * Q // P
CC = C // P
HD = H * D
K8 = 8
KG = K // K8
GROUPS = B * KG
COLS = H * K
E, F = 8, 1024
FC = F // P
CAP = B * Q // E
ST = CAP // P
ROUNDS, BITS = 8, 4
TH = 2 ** BITS - 1
DIRECT = 2
BASE = 2.0 ** 23
BASE_BITS = 0x4B000000
LO = 16
EPS = 1e-5
WARM = 12
TAKEN = -3.0e38

C_ID, C_TRI, C_I8, C_IOTA, C_TOK, C_SM, C_EX, C_W, C_END = 0, 128, 256, 264, 280, 312, 328, 456, 584


def build(nc, x, ctxT, wqT, wk, wv, wo, wth1, wth2T, centT, gb, w1, b1, w2, b2, consts, iconsts, out):
    f32, f32r, bf16, i32 = mybir.dt.float32, mybir.dt.float32r, mybir.dt.bfloat16, mybir.dt.int32
    ALU, ACT, AX = mybir.AluOpType, mybir.ActivationFunctionType, mybir.AxisListType
    ds = bass.ds
    rows_dram = nc.dram_tensor("rows_scratch", (B * Q, 2 * C), f32, kind="Internal").ap()

    with ExitStack() as top:
        def sb(name, shape, dt=f32, ctx=top):
            return ctx.enter_context(nc.sbuf_tensor(name, shape, dt))

        def sem(name):
            return top.enter_context(nc.semaphore(name))

        bank = [top.enter_context(nc.psum_tensor(f"bank{i}", [P, 512], f32)) for i in range(8)]

        cst = sb("cst", [P, C_END])
        ics = sb("ics", [P, ROUNDS * TH + 1], i32)
        tri_b = sb("tri_b", [P, P], bf16)
        ones_b = sb("ones_b", [P, 4 * P], bf16)
        cent = sb("cent", [P, CC, E])
        gbs = sb("gbs", [P, 2, CC])
        b1s = sb("b1s", [P, E * FC])
        b2s = sb("b2s", [P, E, C])
        mhalf = sb("mhalf", [P, T])
        ident = cst[:, C_ID:C_ID + P]
        iota = cst[:, C_IOTA:C_IOTA + LO]
        tok = cst[:, C_TOK:C_TOK + 2 * T].rearrange("p (t a) -> p t a", a=2)
        smask = cst[:, C_SM:C_SM + LO]
        expand = cst[0:LO, C_EX:C_EX + P]
        step_w = cst[:, C_W:C_W + ROUNDS * (TH + 1)].rearrange("p (r j) -> p r j", r=ROUNDS)

        xs = sb("xs", [P, T, C])
        Am = sb("Am", [P, 2, B, CC, COLS], f32r)
        Bm = sb("Bm", [P, 2, GROUPS, C], f32r)
        bst = sb("bst", [P, T, 6])
        mv1 = sb("mv1", [P, T, 2])
        r1 = sb("r1", [P, T])
        nmr = sb("nmr", [P, T])
        mxh = sb("mxh", [P, 2, 2, H])
        mx = sb("mx", [P, 2, H])
        sm = sb("sm", [P, 2, H])
        rs = sb("rs", [P, 2, H])
        bst2 = sb("bst2", [P, 2, 6])
        mv2 = sb("mv2", [P, 2, 2])
        sc = sb("sc", [P, 2, 8])
        S = sb("S", [P, E, T])

        M = sb("M", [P, T])
        pen = sb("pen", [P, T])
        Mpre = sb("Mpre", [P, T])
        cmpb = sb("cmpb", [P, TH, T], bf16)
        cntb = sb("cntb", [P, TH + 1], bf16)
        ok = sb("ok", [P, TH + 1])
        acc = sb("acc", [P, 1])
        shi = sb("shi", [P, 1], i32)
        neg = sb("neg", [P, 1], i32)
        bits = sb("bits", [P, 2], i32)
        pre = sb("pre", [P, TH], i32)
        cand = sb("cand", [P, TH], i32)
        GE = sb("GE", [P, 2 * T], bf16)
        INC = sb("INC", [P, 2 * T], bf16)
        one_b = sb("one_b", [P, 2 * T], bf16)
        SEL = sb("SEL", [P, T])
        SLT = sb("SLT", [P, 2 * T])
        slot = sb("slot", [P, T], i32)
        shl = sb("shl", [P, 2, T], i32)
        Loh = sb("Loh", [P, T, LO], bf16)
        Hoh = sb("Hoh", [P, T, LO])
        Htk = sb("Htk", [P, T, 2, LO], bf16)
        Rt = sb("Rt", [LO, 2 * LO])
        Rx = sb("Rx", [P, LO])
        idf = sb("idf", [P, 2, ST])
        idx = sb("idx", [P, 2, ST], i32)

        xn = sb("xn", [P, 2, C])
        xnT = sb("xnT", [P, 2, 2, C], f32r)

        with ExitStack() as prep:
            wrep = sb("wrep", [P, 2, H], f32, prep)
            mix = sb("mix", [P, 2, H, K8], f32, prep)
            ctx_s = sb("ctx_s", [P, CC, B * K], f32, prep)
            wqT_s = sb("wqT_s", [P, HD // P, C], f32, prep)
            wo_s = sb("wo_s", [P, HD // P, C], f32, prep)
            kvT = sb("kvT", [P, 2, HD // P, 2, B * K], f32, prep)
            AB = sb("AB", [P, 2, CC, GROUPS, H, K8], f32, prep)
            with ExitStack() as early:
                wk_s = sb("wk_s", [P, CC, HD], f32, early)
                wv_s = sb("wv_s", [P, CC, HD], f32, early)
            ABT = sb("ABT", [P, 2, GROUPS, C], f32, prep)
        G = sb("G", [P, 2, ST, 2 * C])
        yF = sb("yF", [P, CC, CAP])
        yT = sb("yT", [P, 2, 2, CC, CAP], f32r)
        w1s = sb("w1s", [P, CC, F])
        w2s = sb("w2s", [P, 2, FC, C])
        hT = sb("hT", [P, 2, FC, CAP])
        with ExitStack() as tiles:
            pr = sb("pr", [P, 2, COLS], f32, tiles)
            pT = sb("pT", [P, 2, 2, COLS], f32r, tiles)
            x1 = sb("x1", [P, 2, C], f32, tiles)
            row = sb("row", [P, 2, 2 * C], f32, tiles)
            yTs = sb("yTs", [P, 2, C], f32, tiles)
        w1p = sb("w1p", [P, 2, 2, CC, F], f32r)

        s_in = {n: sem("in_" + n) for n in ("cst", "ctx", "wk", "wv", "wq", "wo", "rep", "small", "x")}
        s_consts, s_ones, s_zero, s_mix = sem("consts_made"), sem("ones_made"), sem("zeros_made"), sem("mix_made")
        s_fill, s_evA, s_evD = sem("bank_filled"), sem("filled_copied_act"), sem("filled_copied_dve")
        s_bn1, s_mv1, s_ve1, s_r1 = sem("x_stats"), sem("x_mean_var"), sem("x_var_eps"), sem("x_rstd")
        s_nmr, s_xn, s_xT = sem("x_minus_mean_rstd"), sem("xn_made"), sem("xn_transposed")
        s_xTh, s_xTs = sem("xnT_high"), sem("xnT_rest")
        s_lg, s_mx, s_sub, s_exp = sem("logits_made"), sem("max_made"), sem("max_subtracted"), sem("exp_made")
        s_sum, s_rc, s_pn = sem("sum_made"), sem("recip_made"), sem("probs_made")
        s_pT, s_pTh, s_pTs = sem("probs_transposed"), sem("probsT_high"), sem("probsT_rest")
        s_pv, s_x1, s_bn2, s_mv2 = sem("attn_made"), sem("x1_made"), sem("x1_stats"), sem("x1_mean_var")
        s_ln, s_yn, s_res = sem("ln_steps"), sem("yn_made"), sem("residual_made")
        s_row = [sem("row_stored_even"), sem("row_stored_odd")]
        s_yT, s_yTs, s_scp, s_sc = sem("yn_transposed"), sem("ynT_copied"), sem("scores_in_psum"), sem("scores_made")
        r_m, r_cmp, r_cnt, r_tot = sem("masked_scores"), sem("compared"), sem("counted"), sem("totals_made")
        r_j, r_int, r_neg, r_bits, r_pre, r_cand = (sem("r_" + n) for n in ("sum", "sum_int", "neg", "bits", "kept_bits", "cand"))
        r_ge, r_inc, r_rank, r_sel = sem("r_ge"), sem("r_inc"), sem("r_rank"), sem("r_sel")
        r_slt, r_slot, r_hl, r_pen1, r_pen, r_mpre = (sem("r_" + n) for n in ("slt", "slot", "hl", "pen1", "pen", "mpre"))
        r_loh, r_hoh, r_htk = sem("r_loh"), sem("r_hoh"), sem("r_htk")
        r_R, r_Rt, r_Rx, r_Rxm = sem("r_R"), sem("r_Rt"), sem("r_Rx"), sem("r_Rxm")
        r_idf, r_idx = sem("r_idf"), sem("r_idx")
        e_w1, e_w1h, e_w1l = sem("w1_loaded"), sem("w1_high"), sem("w1_rest")
        e_w2 = [sem("w2_even"), sem("w2_odd")]
        e_g = [sem(f"gathered{i}") for i in range(4)]
        e_gT, e_yT, e_yl, e_h, e_hs = sem("rows_transposed"), sem("rowsT_copied"), sem("rowsT_rest"), sem("hidden_in_psum"), sem("hidden_made")
        e_o, e_rb, e_fin = sem("expert_out"), sem("residual_bias"), sem("rows_final")
        e_out = [sem(f"rows_scattered{i}") for i in range(4)]

        block = top.enter_context(nc.Block())

        def wait(eng, s, val):
            if isinstance(val, int) and val <= 0:
                return
            eng.wait_ge(s, val)

        def wait_alone(eng, s, val):
            wait(eng, s, val)
            if not isinstance(val, int):
                eng.nop(nofuse=True)

        def steps(eng, first, loop_from, loop_to, last, step):
            for i in range(first, loop_from):
                step(i, i % 2)
            with eng.Fori(loop_from, loop_to - 1, 2) as i:
                step(i, loop_from % 2)
                step(i + 1, 1 - loop_from % 2)
            for i in range(loop_to, last):
                step(i, i % 2)

        def live(t, n=T):
            return not isinstance(t, int) or 0 <= t < n

        def searches(k):
            return live(k, E - 1)

        def par(t, u, lag):
            return (u - lag) % 2

        A_FIRST, A_LOOP, A_LOOP_END, A_LAST = -2, 7, 13, T + 7
        R_FIRST, R_LOOP, R_LOOP_END, R_LAST = 0, 3, 7, E + 2

        MIXED, LATE, FILLS = 36, 46, 52

        def late(s):
            return {0: range(LATE, LATE + 3), 1: range(LATE + 3, FILLS)}.get(s, ()) if isinstance(s, int) else ()

        def fill_bank(f):
            return bank[f % 8 if f < LATE else 4 + (f - LATE) % 3]

        def wait_copied(eng, f):
            if f < MIXED:
                wait(eng, s_evA, f // 2 + 1)
                wait(eng, s_evD, (f + 1) // 2)
            else:
                wait(eng, s_evD, MIXED // 2 + f - MIXED + 1)

        def copy_fill(f, copy):
            src = bank[f % 8]
            if f < 4:
                side, g = f // 2, f % 2
                for o in range(2):
                    q = slice(o * D, (o + 1) * D)
                    last = copy(kvT[q, side, 4 * g:4 * g + 4, o, :], src[q].rearrange("p (j n) -> p j n", j=4),
                                1.0 if side else D ** -0.5)
            elif f < 20:
                side, g = (f - 4) // 8, (f - 4) % 8
                cc, h = g // 4, g % 4 * 4
                last = copy(AB[:, side, cc, :, h:h + 4, :].rearrange("p g h k -> p h g k"),
                            src[:].rearrange("p (h g k) -> p h g k", h=4, g=GROUPS), 1.0)
            else:
                side, g = (f - 20) // 8, (f - 20) % 8
                last = copy(ABT[:, side, 2 * g:2 * g + 2, :], src[:].rearrange("p (g c) -> p g c", g=2), 1.0)
            return last

        def mixed(f, part):
            side, g = (f - MIXED) // 8, (f - MIXED) % 8
            if side == 0:
                return Am[:, part, g // 4, g % 4 // 2, (g % 2) * 512:(g % 2 + 1) * 512]
            return Bm[:, part, 2 * g:2 * g + 2, :].rearrange("p g c -> p (g c)")

        @block.sync
        def _(sp):
            sp.dma_start(ctx_s[:], ctxT.rearrange("(c p) n -> p c n", p=P)).then_inc(s_in["ctx"], 16)
            sp.dma_start(wk_s[:], wk.rearrange("(c p) n -> p c n", p=P)).then_inc(s_in["wk"], 16)
            sp.dma_start(wv_s[:], wv.rearrange("(c p) n -> p c n", p=P)).then_inc(s_in["wv"], 16)
            sp.dma_start(wqT_s[:], wqT.rearrange("(j p) n -> p j n", p=P)).then_inc(s_in["wq"], 16)
            sp.dma_start(cst[:], consts).then_inc(s_in["cst"], 16)
            sp.dma_start(wo_s[:], wo.rearrange("(j p) n -> p j n", p=P)).then_inc(s_in["wo"], 16)
            sp.dma_start(xs[:], x.rearrange("(t p) c -> p t c", p=P)).then_inc(s_in["x"], 16)
            sp.dma_start(ics[:], iconsts).then_inc(s_in["small"], 16)
            sp.dma_start(cent[:], centT.rearrange("(c p) e -> p c e", p=P)).then_inc(s_in["small"], 16)
            sp.dma_start(gbs[:], gb.rearrange("p (a c) -> p a c", a=2)).then_inc(s_in["small"], 16)
            sp.dma_start(b1s[:], b1).then_inc(s_in["small"], 16)
            sp.dma_start(b2s[:], b2.unsqueeze(0).to_broadcast([P, E, C])).then_inc(s_in["small"], 16)

            sp.wait_ge(s_fill, FILLS)
            wait_copied(sp, FILLS - 1)
            sp.dma_start(w1s[:], w1[0].rearrange("(c p) f -> p c f", p=P)).then_inc(e_w1, 16)
            for e in range(2):
                sp.dma_start(w2s[:, e], w2[e].rearrange("(c p) f -> p c f", p=P)).then_inc(e_w2[e], 16)

            def store_row(s, u):
                t = s - 5
                if live(t):
                    v = par(t, u, 5)
                    wait(sp, s_yn, t + 1)
                    wait(sp, s_res, t + 1)
                    sp.dma_start(rows_dram[ds(t * P, P), :], row[:, v, :]).then_inc(s_row[v], 16)
            steps(sp, A_FIRST, A_LOOP, A_LOOP_END, A_LAST + 1, store_row)

            def load_w(k, u):
                wait(sp, e_w1l, CC * k)
                sp.dma_start(w1s[:], w1[ds(k, 1)].rearrange("e (c p) f -> p (e c) f", p=P)).then_inc(e_w1, 16)
                if not isinstance(k, int) or k > 1:
                    wait(sp, e_o, ST * (k - 1))
                    sp.dma_start(w2s[:, u], w2[ds(k, 1)].rearrange("e (c p) f -> p (e c) f", p=P)).then_inc(e_w2[u], 16)
            load_w(1, 1)
            steps(sp, 2, 2, 8, 8, load_w)

        @block.gpsimd
        def _(pool):
            for o in range(2):
                nc.gpsimd.memset(kvT[o * D:(o + 1) * D, :, :, 1 - o, :], 0.0).then_inc(s_zero, 1)
                pool.wait_ge(s_zero, o + 1)
            for o, src in ((0, wth1), (1, wth2T)):
                for k in range(K8):
                    pool.dma_start(wrep[k:P:K8, o, :], src).then_inc(s_in["rep"], 16)
            nc.gpsimd.memset(mhalf[:], -0.5).then_inc(s_consts, 1)
            nc.gpsimd.memset(pen[:], 0.0).then_inc(s_consts, 1)
            nc.gpsimd.memset(one_b[:], 1.0).then_inc(s_consts, 1)
            nc.gpsimd.memset(cntb[:, TH:], float(T)).then_inc(s_consts, 1)
            pool.wait_ge(s_consts, 4)
            pool.wait_ge(s_ve1, 1)
            nc.gpsimd.tensor_tensor(r1[:], r1[:], mhalf[:], ALU.pow).then_inc(s_r1, 1)

            def attn(s, u):
                t = s - 1
                if live(t):
                    v = par(t, u, 1)
                    wait(pool, s_exp, t + 1)
                    wait_alone(pool, s_rc, t + 1)
                    p4 = pr[:, v, :].rearrange("p (g i k) -> p g i k", g=KG, i=H)
                    pool_mul = nc.gpsimd.tensor_tensor(
                        p4, p4, rs[:, v, :].unsqueeze(1).unsqueeze(3).to_broadcast([P, KG, H, K8]), ALU.mult)
                    pool_mul.then_inc(s_pn, 1)
                t = s - 3
                if live(t):
                    v = par(t, u, 3)
                    c = [sc[:, v, n:n + 1] for n in range(8)]
                    m, var = mv2[:, v, 0:1], mv2[:, v, 1:2]
                    wait(pool, s_mv2, t + 1)
                    wait(pool, s_yn, t - 1)
                    wait_alone(pool, s_res, t - 1)
                    n = 9 * t
                    nc.gpsimd.tensor_scalar(c[0], var, 1.0, EPS, ALU.mult, ALU.add).then_inc(s_ln, 1)
                    wait_alone(pool, s_ln, n + 1)
                    nc.gpsimd.tensor_tensor(c[1], c[0], mhalf[:, 0:1], ALU.pow).then_inc(s_ln, 1)
                    wait_alone(pool, s_ln, n + 2)
                    nc.gpsimd.tensor_scalar(c[2], var, c[1], c[1], ALU.mult, ALU.mult).then_inc(s_ln, 1)
                    wait_alone(pool, s_ln, n + 3)
                    nc.gpsimd.tensor_scalar(c[3], c[2], 1.0, EPS, ALU.mult, ALU.add).then_inc(s_ln, 1)
                    wait_alone(pool, s_ln, n + 4)
                    nc.gpsimd.tensor_tensor(c[4], c[3], mhalf[:, 0:1], ALU.pow).then_inc(s_ln, 1)
                    wait_alone(pool, s_ln, n + 5)
                    nc.gpsimd.tensor_scalar(c[5], c[4], c[1], 1.0, ALU.mult, ALU.mult).then_inc(s_ln, 1)
                    wait_alone(pool, s_ln, n + 6)
                    nc.gpsimd.tensor_scalar(c[6], m, c[5], -1.0, ALU.mult, ALU.mult).then_inc(s_ln, 1)
                    nc.gpsimd.tensor_scalar(c[7], m, c[1], -1.0, ALU.mult, ALU.mult).then_inc(s_ln, 1)
                    nc.gpsimd.tensor_scalar(c[3], c[1], 1.0, 1.0, ALU.mult, ALU.add).then_inc(s_ln, 1)
            steps(pool, A_FIRST, A_LOOP, A_LOOP_END, A_LAST, attn)

            for v in range(2):
                pool.wait_ge(s_row[v], 16 * T // 2)
            pool.wait_ge(s_in["small"], 80)

            def token_rows(e):
                wait(pool, r_hoh, e + 1)
                wait_alone(pool, r_R, e)
                nc.gpsimd.tensor_tensor(Htk[:], Hoh[:].unsqueeze(2).to_broadcast([P, T, 2, LO]),
                                        tok.unsqueeze(3).to_broadcast([P, T, 2, LO]), ALU.mult).then_inc(r_htk, 1)

            def gather(e, v):
                wait(pool, r_idx, e + 1)
                for a in range(ST):
                    wait_alone(pool, e_out[2 * v + a], 16 * (e // 2))
                for a in range(ST):
                    pool.indirect_dma_start(
                        out=G[:, v, a, :], out_offset=None, in_=rows_dram,
                        in_offset=bass.IndirectOffsetOnAxis(ap=idx[:, v, a:a + 1], axis=0),
                    ).then_inc(e_g[2 * v + a], 16)

            def w1_rest(e, v, c):
                wait(pool, e_w1h, e + 1)
                wait_alone(pool, e_h, FC // 2 * (e - 1))
                nc.gpsimd.tensor_tensor(w1p[:, 1, v, c], w1s[:, c], w1p[:, 0, v, c].bitcast(f32), ALU.subtract).then_inc(e_w1l, 1)

            def y_rest(e, v):
                for c in range(CC):
                    wait_alone(pool, e_yT, 4 * e + 2 * c + 2)
                    nc.gpsimd.tensor_tensor(yT[:, 1, v, c, :], yF[:, c, :], yT[:, 0, v, c, :].bitcast(f32),
                                            ALU.subtract).then_inc(e_yl, 1)

            def bias(e, v, h):
                for a in range(ST):
                    wait_alone(pool, e_g[2 * v + a], 16 * h)
                    nc.gpsimd.tensor_tensor(G[:, v, a, C:], G[:, v, a, C:],
                                            b2s[:, ds(e, 1), :].rearrange("p e c -> p (e c)"), ALU.add).then_inc(e_rb, 1)

            def scatter(e, v):
                for a in range(ST):
                    wait_alone(pool, e_fin, ST * e + a + 1)
                    pool.indirect_dma_start(
                        out=out, out_offset=bass.IndirectOffsetOnAxis(ap=idx[:, v, a:a + 1], axis=0),
                        in_=G[:, v, a, C:], in_offset=None).then_inc(e_out[2 * v + a], 16)

            def experts(k, u):
                if live(k - 1, E):
                    v = 1 - u
                    token_rows(k - 1)
                    w1_rest(k - 1, v, 0)
                    gather(k - 1, v)
                    w1_rest(k - 1, v, 1)
                    bias(k - 1, v, (k + 1) // 2)
                    y_rest(k - 1, v)
                if live(k - 2, E):
                    scatter(k - 2, u)
            steps(pool, R_FIRST, R_LOOP, R_LOOP_END, R_LAST, experts)
            for i in range(4):
                pool.wait_ge(e_out[i], 16 * E // 2)

        @block.scalar
        def _(act):
            def normalize(t, v):
                nc.scalar.activation(xn[:, v, :], xs[:, ds(t, 1), :].rearrange("p t c -> p (t c)"), ACT.Identity,
                                     scale=r1[:, ds(t, 1)], bias=nmr[:, ds(t, 1)]).then_inc(s_xn, 1)

            def mixed_high(f):
                act.wait_ge(s_fill, f + 1)
                nc.scalar.activation(mixed(f, 0), fill_bank(f)[:], ACT.Copy).then_inc(s_evA, 1)

            for f in range(LATE):
                if f == MIXED:
                    act.wait_ge(s_nmr, 1)
                    normalize(0, 0)
                    normalize(1, 1)
                if f >= MIXED:
                    mixed_high(f)
                elif f % 2 == 0:
                    act.wait_ge(s_fill, f + 1)
                    copy_fill(f, lambda to, src, scale: nc.scalar.activation(to, src, ACT.Copy, scale=scale)).then_inc(s_evA, 1)
            act.wait_ge(s_in["small"], 80)

            def attn(s, u):
                t = s + 1
                if live(t):
                    v = par(t, u, -1)
                    wait(act, s_xT, t + 1)
                    wait(act, s_lg, t - 1)
                    nc.scalar.activation(xnT[:, 0, v, :], bank[7][:, 0:C], ACT.Copy).then_inc(s_xTh, 1)
                t = s - 1
                if live(t):
                    v = par(t, u, 1)
                    wait(act, s_sub, 2 * t + 2)
                    nc.scalar.activation(pr[:, v, :], pr[:, v, :], ACT.Exp).then_inc(s_exp, 1)
                t = s - 2
                if live(t):
                    v = par(t, u, 2)
                    wait(act, s_pv, t - 1)
                    for g in range(2):
                        wait(act, s_pT, 2 * t + g + 1)
                        nc.scalar.activation(pT[:, 0, v, g * 512:(g + 1) * 512], bank[4 + g][:], ACT.Copy).then_inc(s_pTh, 1)
                t = s + 2
                if live(t) and not (isinstance(s, int) and s < 0):
                    wait(act, s_xT, t - 1)
                    normalize(t, par(t, u, -2))
                for f in late(s):
                    mixed_high(f)
                t = s - 4
                if live(t):
                    v = par(t, u, 4)
                    wait(act, s_ln, 9 * t + 7)
                    wait(act, s_x1, t + 1)
                    wait(act, s_row[v], 16 * (t // 2))
                    wait(act, s_yT, t - 1)
                    nc.scalar.activation(row[:, v, 0:C], x1[:, v, :], ACT.Identity, scale=sc[:, v, 5:6],
                                         bias=sc[:, v, 6:7]).then_inc(s_yn, 1)
                    wait(act, s_ln, 9 * t + 9)
                    nc.scalar.activation(row[:, v, C:], x1[:, v, :], ACT.Identity, scale=sc[:, v, 3:4],
                                         bias=sc[:, v, 7:8]).then_inc(s_res, 1)
                t = s - 5
                if live(t):
                    v = par(t, u, 5)
                    wait(act, s_yT, t + 1)
                    wait(act, s_scp, t - 1)
                    for c in range(CC):
                        nc.scalar.activation(yTs[:, v, c * P:(c + 1) * P], bank[7][:, c * P:(c + 1) * P], ACT.Identity,
                                             scale=gbs[:, 0, c:c + 1], bias=gbs[:, 1, c:c + 1]).then_inc(s_yTs, 1)
            steps(act, A_FIRST, A_LOOP, A_LOOP_END, A_LAST, attn)

            def w1_high(e, v):
                wait(act, e_w1, 16 * (e + 1))
                wait(act, e_h, FC // 2 * (e - 1))
                nc.scalar.activation(w1p[:, 0, v], w1s[:], ACT.Copy).then_inc(e_w1h, 1)

            def rows(e, v):
                wait(act, e_gT, e + 1)
                wait(act, e_yl, CC * e)
                for c in range(CC):
                    for to in (yF[:, c, :], yT[:, 0, v, c, :]):
                        nc.scalar.activation(to, bank[0][:, c * CAP:(c + 1) * CAP], ACT.Identity,
                                             scale=gbs[:, 0, c:c + 1], bias=gbs[:, 1, c:c + 1]).then_inc(e_yT, 1)

            def hidden(e, v, g):
                wait(act, e_h, FC // 2 * e + g + 1)
                for h in range(2):
                    f = 2 * g + h
                    nc.scalar.activation(hT[:, v, f, :], bank[1 + g % 3][:, h * CAP:(h + 1) * CAP], ACT.Gelu_apprx_tanh,
                                         bias=b1s[:, ds(e * FC + f, 1)]).then_inc(e_hs, 1)

            def experts(k, u):
                if live(k - 2, E):
                    wait(act, e_o, ST * (k - 2))
                    for g in range(FC // 2 - 1):
                        hidden(k - 2, u, g)
                if live(k - 1, E):
                    v = 1 - u
                    wait(act, r_R, k)
                    nc.scalar.activation(Rt[:], bank[7][0:LO, 0:2 * LO], ACT.Copy).then_inc(r_Rt, 1)
                if live(k - 2, E):
                    hidden(k - 2, u, FC // 2 - 1)
                if live(k - 1, E):
                    wait(act, e_h, FC // 2 * (k - 2))
                    rows(k - 1, v)
                if live(k, E):
                    w1_high(k, u)
            act.wait_ge(s_sc, T)
            for v in range(2):
                act.wait_ge(s_row[v], 16 * T // 2)
            steps(act, R_FIRST, R_LOOP, R_LOOP_END, R_LAST, experts)

        @block.vector
        def _(dve):
            nc.vector.memset(ones_b[:], 1.0).then_inc(s_ones, 1)

            def mixed_rest(f):
                dve.wait_ge(s_evA, MIXED // 2 + f - MIXED + 1)
                nc.vector.tensor_tensor(mixed(f, 1), fill_bank(f)[:], mixed(f, 0).bitcast(f32), ALU.subtract).then_inc(s_evD, 1)

            for f in range(LATE):
                if f >= MIXED:
                    mixed_rest(f)
                elif f % 2 == 1:
                    dve.wait_ge(s_fill, f + 1)
                    copy_fill(f, lambda to, src, scale: nc.vector.tensor_scalar(to, src, scale, None, ALU.mult)).then_inc(s_evD, 1)
                if f in (11, 15):
                    dve.wait_ge(s_in["x"], 16)
                    for t in range(T // 2):
                        t += T // 2 if f == 15 else 0
                        nc.vector.bn_stats(bst[:, t, :], xs[:, t, :]).then_inc(s_bn1, 1)
                if f == 15:
                    dve.wait_ge(s_in["cst"], 16)
                    dve.wait_ge(s_in["rep"], 16 * 2 * K8)
                    for o in range(2):
                        nc.vector.tensor_tensor(mix[:, o], wrep[:, o, :].unsqueeze(2).to_broadcast([P, H, K8]),
                                                cst[:, C_I8:C_I8 + K8].unsqueeze(1).to_broadcast([P, H, K8]),
                                                ALU.mult).then_inc(s_mix, 1)
                    nc.vector.tensor_copy(tri_b[:], cst[:, C_TRI:C_TRI + P]).then_inc(s_mix, 1)
                if f == 19:
                    for t in range(T):
                        dve.wait_ge(s_bn1, t + 1)
                        nc.vector.bn_aggr(mv1[:, t, :], bst[:, t, :]).then_inc(s_mv1, 1)
                    dve.wait_ge(s_mv1, T)
                    nc.vector.tensor_scalar(r1[:], mv1[:, :, 1], EPS, None, ALU.add).then_inc(s_ve1, 1)
                if f == 29:
                    dve.wait_ge(s_r1, 1)
                    nc.vector.scalar_tensor_tensor(nmr[:], mv1[:, :, 0], -1.0, r1[:], ALU.mult, ALU.mult).then_inc(s_nmr, 1)

            def attn(s, u):
                t = s - 3
                if live(t):
                    v = par(t, u, 3)
                    wait(dve, s_pv, t + 1)
                    wait(dve, s_yn, t - 1)
                    wait(dve, s_res, t - 1)
                    nc.vector.tensor_tensor(x1[:, v, :], bank[6][:, 0:C],
                                            xs[:, ds(t, 1), :].rearrange("p t c -> p (t c)"), ALU.add).then_inc(s_x1, 1)
                t = s - 7
                if live(t):
                    wait(dve, s_scp, t + 1)
                    if not live(s - 3):
                        wait(dve, s_pv, T)
                    nc.vector.tensor_copy(S[:, :, ds(t, 1)].rearrange("p e t -> p (e t)"),
                                          bank[6][:, C:C + E]).then_inc(s_sc, 1)
                t = s + 1
                if live(t):
                    v = par(t, u, -1)
                    wait(dve, s_xTh, t + 1)
                    nc.vector.tensor_tensor(xnT[:, 1, v, :], bank[7][:, 0:C], xnT[:, 0, v, :].bitcast(f32),
                                            ALU.subtract).then_inc(s_xTs, 1)
                t = s - 3
                if live(t):
                    v = par(t, u, 3)
                    wait(dve, s_x1, t + 1)
                    nc.vector.bn_stats(bst2[:, v, :], x1[:, v, :]).then_inc(s_bn2, 1)
                t = s - 1
                if live(t):
                    v = par(t, u, 1)
                    wait(dve, s_exp, t + 1)
                    nc.vector.tensor_reduce(sm[:, v, :], pr[:, v, :].rearrange("p (g i k) -> p i g k", g=KG, i=H),
                                            AX.XY, ALU.add).then_inc(s_sum, 1)
                t = s - 2
                if live(t):
                    v = par(t, u, 2)
                    q = slice(0, 512)
                    wait(dve, s_pTh, 2 * t + 1)
                    nc.vector.tensor_tensor(pT[:, 1, v, q], bank[4][:], pT[:, 0, v, q].bitcast(f32),
                                            ALU.subtract).then_inc(s_pTs, 1)
                t = s - 1
                if live(t):
                    v = par(t, u, 1)
                    wait(dve, s_sum, t + 1)
                    wait(dve, s_pn, t - 1)
                    nc.vector.reciprocal(rs[:, v, :], sm[:, v, :]).then_inc(s_rc, 1)
                t = s - 3
                if live(t):
                    v = par(t, u, 3)
                    wait(dve, s_bn2, t + 1)
                    wait_alone(dve, s_ln, 9 * (t - 1))
                    nc.vector.bn_aggr(mv2[:, v, :], bst2[:, v, :]).then_inc(s_mv2, 1)
                t = s - 2
                if live(t):
                    v = par(t, u, 2)
                    q = slice(512, 1024)
                    wait(dve, s_pTh, 2 * t + 2)
                    nc.vector.tensor_tensor(pT[:, 1, v, q], bank[5][:], pT[:, 0, v, q].bitcast(f32),
                                            ALU.subtract).then_inc(s_pTs, 1)
                t = s
                if live(t):
                    v = par(t, u, 0)
                    lg = [bank[2 * v][:], bank[2 * v + 1][:]]
                    wait(dve, s_lg, t + 1)
                    for g in range(2):
                        nc.vector.tensor_reduce(mxh[:, v, g, :], lg[g].rearrange("p (g i k) -> p i g k", i=H, k=K8),
                                                AX.XY, ALU.max).then_inc(s_mx, 1)
                    wait(dve, s_mx, 3 * t + 2)
                    nc.vector.tensor_tensor(mx[:, v, :], mxh[:, v, 0, :], mxh[:, v, 1, :], ALU.max).then_inc(s_mx, 1)
                    wait(dve, s_mx, 3 * t + 3)
                    wait(dve, s_pT, 2 * (t - 1))
                    for g in range(2):
                        nc.vector.tensor_tensor(
                            pr[:, v, g * 512:(g + 1) * 512].rearrange("p (g i k) -> p g i k", i=H, k=K8),
                            lg[g].rearrange("p (g i k) -> p g i k", i=H, k=K8),
                            mx[:, v, :].unsqueeze(1).unsqueeze(3).to_broadcast([P, KG // 2, H, K8]),
                            ALU.subtract).then_inc(s_sub, 1)
                for f in late(s):
                    mixed_rest(f)
            steps(dve, A_FIRST, A_LOOP, A_LOOP_END, A_LAST, attn)

            dve.wait_ge(s_sc, T)
            dve.wait_ge(s_consts, 4)
            nc.vector.tensor_copy(M[:], S[:, 0, :]).then_inc(r_m, 1)

            def compare(k, r):
                thr = (ics[:, 0:TH] if r == 0 else cand[:]).bitcast(f32)
                wait(dve, r_m, k + 1)
                if r > 0:
                    wait(dve, r_cand, (ROUNDS - 1) * k + r)
                nc.vector.tensor_tensor(cmpb[:], M[:].unsqueeze(1).to_broadcast([P, TH, T]),
                                        thr.unsqueeze(2).to_broadcast([P, TH, T]), ALU.is_ge).then_inc(r_cmp, 1)

            def count(k, r):
                wait(dve, r_cmp, ROUNDS * k + r + 1)
                with nc.allow_low_precision(reason="counts of at most 16 are exact in bfloat16"):
                    nc.vector.tensor_reduce(cntb[:, 0:TH], cmpb[:], AX.X, ALU.add).then_inc(r_cnt, 1)

            def keep(k, r):
                if r > 0:
                    a = (r + 1) % 2
                    wait(dve, r_bits, ROUNDS * k + r)
                    if r < ROUNDS - 1:
                        nc.vector.tensor_scalar(pre[:], ics[:, (r + 1) * TH:(r + 2) * TH], bits[:, a:a + 1], None,
                                                ALU.bitwise_xor).then_inc(r_pre, 1)
                    else:
                        nc.vector.tensor_tensor(pre[:, 0:1], ics[:, ROUNDS * TH:], bits[:, a:a + 1],
                                                ALU.bitwise_xor).then_inc(r_pre, 1)

            def narrow(k, r, v):
                between = r == 3 and live(k - 1, E)
                n = ROUNDS * k + r
                a, b = (r + 1) % 2, r % 2
                wait(dve, r_tot, n + 1)
                nc.vector.scalar_tensor_tensor(ok[:], bank[6][:, 0:TH + 1], float(CAP), step_w[:, r, :], ALU.is_ge,
                                               ALU.mult, accum_out=acc[:]).then_inc(r_j, 1)
                if between:
                    indices(k - 1, v, 0)
                wait(dve, r_j, n + 1)
                if r < DIRECT:
                    nc.vector.tensor_copy(shi[:], acc[:]).then_inc(r_int, 1)
                    new = shi[:]
                else:
                    new = acc[:].bitcast(i32)
                if r == 0:
                    nc.vector.tensor_scalar(neg[:], ok[:, TH // 2:TH // 2 + 1], 0.0, -1.0, ALU.is_ge, ALU.mult).then_inc(r_neg, 1)
                    wait(dve, r_neg, k + 1)
                if r < DIRECT:
                    wait(dve, r_int, DIRECT * k + r + 1)
                if r == 0:
                    nc.vector.tensor_scalar(cand[:], ics[:, TH:2 * TH], neg[:], new,
                                            ALU.bitwise_xor, ALU.bitwise_xor).then_inc(r_cand, 1)
                    nc.vector.tensor_tensor(bits[:, b:b + 1], new, neg[:], ALU.bitwise_xor).then_inc(r_bits, 1)
                else:
                    wait(dve, r_pre, (ROUNDS - 1) * k + r)
                    if r < ROUNDS - 1:
                        nc.vector.tensor_scalar(cand[:], pre[:], new, None, ALU.bitwise_xor).then_inc(r_cand, 1)
                        if between:
                            indices(k - 1, v, 1)
                        nc.vector.tensor_tensor(bits[:, b:b + 1], bits[:, a:a + 1], new, ALU.bitwise_xor).then_inc(r_bits, 1)
                    else:
                        nc.vector.tensor_tensor(bits[:, b:b + 1], pre[:, 0:1], new, ALU.bitwise_xor).then_inc(r_bits, 1)
                if between:
                    indices(k - 1, v, 2)

            def final(e, v, a):
                wait(dve, e_o, ST * e + a + 1)
                wait(dve, e_rb, ST * e + a + 1)
                nc.vector.tensor_tensor(G[:, v, a, C:], bank[4 + a][:, 0:C], G[:, v, a, C:], ALU.add).then_inc(e_fin, 1)

            def select(k):
                if searches(k):
                    th = bits[:, (ROUNDS - 1) % 2:(ROUNDS - 1) % 2 + 1].bitcast(f32)
                    wait(dve, r_bits, ROUNDS * (k + 1))
                    nc.vector.tensor_scalar(GE[:, 0:T], M[:], th, None, ALU.is_gt).then_inc(r_ge, 1)
                    nc.vector.tensor_scalar(GE[:, T:], M[:], th, None, ALU.is_equal).then_inc(r_ge, 1)
                else:
                    wait(dve, r_pen, k)
                    wait(dve, r_rank, k)
                    nc.vector.tensor_scalar(GE[:, 0:T], pen[:], 0.0, None, ALU.is_equal).then_inc(r_ge, 1)
                    nc.vector.tensor_scalar(GE[:, T:], pen[:], 0.0, None, ALU.is_gt).then_inc(r_ge, 1)
                wait(dve, r_ge, 2 * k + 2)
                nc.vector.tensor_tensor_scan(INC[:], one_b[:], GE[:], 0.0, ALU.mult, ALU.add).then_inc(r_inc, 1)
                wait(dve, r_pen, k)
                nc.vector.scalar_tensor_tensor(pen[:], GE[:, 0:T], TAKEN, pen[:], ALU.mult, ALU.add).then_inc(r_pen1, 1)
                wait(dve, r_pen1, k + 1)
                if live(k + 1, E):
                    nc.vector.tensor_tensor(Mpre[:], S[:, ds(k + 1, 1), :].rearrange("p e t -> p (e t)"), pen[:],
                                            ALU.add).then_inc(r_mpre, 1)
                rank = bank[6][:, 32:32 + 2 * T]
                wait(dve, r_rank, k + 1)
                nc.vector.scalar_tensor_tensor(SEL[:], rank[:, T:], float(CAP), GE[:, T:], ALU.is_lt, ALU.mult).then_inc(r_sel, 1)
                nc.vector.scalar_tensor_tensor(SLT[:, 0:T], rank[:, 0:T], 1.0, GE[:, 0:T], ALU.add, ALU.mult).then_inc(r_slt, 1)
                wait(dve, r_sel, k + 1)
                if live(k + 1, E):
                    wait(dve, r_mpre, k + 1)
                    nc.vector.scalar_tensor_tensor(M[:], SEL[:], TAKEN, Mpre[:], ALU.mult, ALU.add).then_inc(r_m, 1)
                nc.vector.scalar_tensor_tensor(SLT[:, T:], rank[:, T:], 1.0, SEL[:], ALU.add, ALU.mult).then_inc(r_slt, 1)

            def slots(k):
                wait(dve, r_slt, 2 * k + 2)
                nc.vector.scalar_tensor_tensor(slot[:], SLT[:, 0:T], -1.0, SLT[:, T:], ALU.add, ALU.add).then_inc(r_slot, 1)
                nc.vector.scalar_tensor_tensor(pen[:], SEL[:], TAKEN, pen[:], ALU.mult, ALU.add).then_inc(r_pen, 1)

            def halves(k):
                wait(dve, r_slot, k + 1)
                nc.vector.tensor_scalar(shl[:, 1, :], slot[:], 4, None, ALU.arith_shift_right).then_inc(r_hl, 1)
                nc.vector.tensor_scalar(shl[:, 0, :], slot[:], 15, None, ALU.bitwise_and).then_inc(r_hl, 1)

            def one_hot(k, half, to, s):
                wait(dve, r_R, k)
                wait(dve, r_hl, 2 * k + 2)
                nc.vector.tensor_tensor(to[:], iota.unsqueeze(1).to_broadcast([P, T, LO]),
                                        shl[:, half, :].unsqueeze(2).to_broadcast([P, T, LO]), ALU.is_equal).then_inc(s, 1)

            def indices(k, v, part):
                if part == 0:
                    wait(dve, r_Rx, k + 1)
                    nc.vector.tensor_tensor(Rx[:], bank[7][:, 32:32 + LO], smask, ALU.mult).then_inc(r_Rxm, 1)
                if part == 1:
                    wait(dve, r_Rxm, k + 1)
                    nc.vector.tensor_reduce(idf[:, v, :], Rx[:].rearrange("p (a b) -> p a b", a=ST), AX.X, ALU.add).then_inc(r_idf, 1)
                if part == 2:
                    for a in range(ST):
                        wait(dve, e_out[2 * v + a], 16 * (k // 2))
                    wait(dve, r_idf, k + 1)
                    nc.vector.tensor_copy(idx[:, v, :], idf[:, v, :]).then_inc(r_idx, 1)

            def experts(k, u):
                for r in range(ROUNDS):
                    if searches(k):
                        compare(k, r)
                        keep(k, r)
                    if r == 0 and live(k - 1, E):
                        slots(k - 1)
                    if searches(k):
                        count(k, r)
                    if r == 0 and live(k - 1, E):
                        halves(k - 1)
                    if r == 1 and live(k - 1, E):
                        one_hot(k - 1, 1, Hoh, r_hoh)
                    if r == 2 and live(k - 1, E):
                        one_hot(k - 1, 0, Loh, r_loh)
                    if r == 2 and live(k, E) and not searches(k):
                        select(k)
                    if r == 3 and live(k - 1, E) and not searches(k):
                        for part in range(3):
                            indices(k - 1, 1 - u, part)
                    if r == 0 and live(k - 3, E) and searches(k - 1):
                        final(k - 3, 1 - u, 1)
                    if r == 6 and live(k - 2, E):
                        final(k - 2, u, 0)
                    if r == 7 and live(k - 2, E) and not searches(k):
                        final(k - 2, u, 1)
                    if searches(k):
                        narrow(k, r, 1 - u)
                if searches(k):
                    select(k)
            steps(dve, R_FIRST, R_LOOP, R_LOOP_END, R_LAST, experts)

        @block.tensor
        def _(pe):
            def mm(out_, l, r, start, stop):
                return nc.tensor.matmul(out_, l, r, start=start, stop=stop)

            def mm3(out_, l, r, start, stop):
                mm(out_, l(0), r(0), start, False)
                mm(out_, l(0), r(1), False, False)
                return mm(out_, l(1), r(0), False, stop)

            pe.wait_ge(s_ones, 1)
            for _ in range(WARM):
                mm(bank[7][:], ones_b[:, 0:P], ones_b[:], True, True)
            pe.wait_ge(s_in["ctx"], 16)
            f = 0
            for w, name in ((wk_s, "wk"), (wv_s, "wv")):
                pe.wait_ge(s_in[name], 16)
                for g in range(2):
                    for j in range(4):
                        for c in range(CC):
                            last = mm(bank[f][:, j * P:(j + 1) * P], w[:, c, (4 * g + j) * P:(4 * g + j + 1) * P],
                                      ctx_s[:, c, :], c == 0, c == CC - 1)
                    last.then_inc(s_fill, 1)
                    f += 1
            pe.wait_ge(s_zero, 2)
            for side, (w, name) in enumerate(((wqT_s, "wq"), (wo_s, "wo"))):
                pe.wait_ge(s_in[name], 16)
                wait_copied(pe, 1 + 2 * side)
                for c in range(CC):
                    if f >= 8:
                        wait_copied(pe, f - 5)
                    for m in range(HD // P):
                        last = mm(bank[(f + m // 2) % 8][:, m % 2 * 2 * P:(m % 2 + 1) * 2 * P],
                                  w[:, m, c * P:(c + 1) * P], kvT[:, side, m].rearrange("p o n -> p (o n)"), True, True)
                    last.then_inc(s_fill, 4)
                    f += 4
            pe.wait_ge(s_in["cst"], 16)
            for side in range(2):
                for g in range(8):
                    wait_copied(pe, max(f - 8, 11 + 8 * side))
                    for h in range(2):
                        for c in range(CC):
                            last = nc.tensor.transpose(bank[f % 8][:, h * C + c * P:h * C + (c + 1) * P],
                                                       AB[:, side, c, 2 * g + h, :, :].rearrange("p h k -> p (h k)"), ident)
                    last.then_inc(s_fill, 1)
                    f += 1
            pe.wait_ge(s_mix, 3)
            def mixed_fill(f):
                side, g = (f - MIXED) // 8, (f - MIXED) % 8
                wait_copied(pe, max(f - (8 if f < LATE else 3), 27 + 8 * side))
                mix_s = mix[:, side].rearrange("p h k -> p (h k)")
                if side == 0:
                    for j in range(4):
                        k, c = g // 4 * KG + g % 2 * 4 + j, g % 4 // 2
                        last = mm(fill_bank(f)[:, j * P:(j + 1) * P], ABT[:, 0, k, c * P:(c + 1) * P], mix_s, True, True)
                else:
                    for j in range(2):
                        last = mm(fill_bank(f)[:, j * C:(j + 1) * C], mix_s, ABT[:, 1, 2 * g + j, :], True, True)
                last.then_inc(s_fill, 1)

            for f in range(MIXED, LATE):
                mixed_fill(f)
            pe.wait_ge(s_in["small"], 80)
            wait_copied(pe, MIXED + 3)

            def attn(s, u):
                t = s + 1
                if live(t):
                    v = par(t, u, -1)
                    wait(pe, s_xn, t + 1)
                    wait(pe, s_xTs, t)
                    wait(pe, s_yTs, 2 * (s - 5))
                    for c in range(CC):
                        last = nc.tensor.transpose(bank[7][:, c * P:(c + 1) * P], xn[:, v, c * P:(c + 1) * P], ident)
                    last.then_inc(s_xT, 1)
                t = s - 2
                if live(t):
                    v = par(t, u, 2)
                    if isinstance(t, int) and t == 0:
                        wait_copied(pe, FILLS - 1)
                    wait(pe, s_pn, t + 1)
                    for g in range(2):
                        wait(pe, s_pTs, 2 * (t - 1) + g + 1)
                        for j in range(4):
                            q = (4 * g + j) * P
                            last = nc.tensor.transpose(bank[4 + g][:, j * P:(j + 1) * P], pr[:, v, q:q + P], ident)
                        last.then_inc(s_pT, 1)
                t = s
                if live(t):
                    v = par(t, u, 0)
                    if isinstance(t, int) and t == 0:
                        wait_copied(pe, LATE - 1)
                    wait(pe, s_xTs, t + 1)
                    wait(pe, s_sub, 2 * (t - 1))
                    for g in range(2):
                        for c in range(CC):
                            last = mm3(bank[2 * v + g][:], lambda i: xnT[:, i, v, c * P:(c + 1) * P],
                                       lambda i: Am[:, i, ds(t // (T // B), 1), c, g * 512:(g + 1) * 512].rearrange(
                                           "p b n -> p (b n)"), c == 0, c == CC - 1)
                    last.then_inc(s_lg, 1)
                for f in late(s):
                    mixed_fill(f)
                t = s - 5
                if live(t):
                    v = par(t, u, 5)
                    wait(pe, s_yn, t + 1)
                    if live(s + 1):
                        wait(pe, s_xTs, s + 2)
                    else:
                        wait(pe, s_yTs, 2 * t)
                    for c in range(CC):
                        last = nc.tensor.transpose(bank[7][:, c * P:(c + 1) * P], row[:, v, c * P:(c + 1) * P], ident)
                    last.then_inc(s_yT, 1)
                t = s - 6
                if live(t):
                    v = par(t, u, 6)
                    wait(pe, s_yTs, 2 * t + 2)
                    wait(pe, s_x1, min(s - 2, T) if isinstance(s, int) else s - 2)
                    wait(pe, s_sc, t)
                    for c in range(CC):
                        last = mm(bank[6][:, C:C + E], yTs[:, v, c * P:(c + 1) * P], cent[:, c, :], c == 0, c == CC - 1)
                    last.then_inc(s_scp, 1)
                t = s - 2
                if live(t):
                    v = par(t, u, 2)
                    wait(pe, s_x1, t)
                    for g in range(KG):
                        wait(pe, s_pTs, 2 * t + g // 4 + 1)
                        last = mm3(bank[6][:, 0:C], lambda i: pT[:, i, v, g * P:(g + 1) * P],
                                   lambda i: Bm[:, i, ds(t // (T // B) * KG + g, 1), :].rearrange("p g c -> p (g c)"),
                                   g == 0, g == KG - 1)
                    last.then_inc(s_pv, 1)
            steps(pe, A_FIRST, A_LOOP, A_LOOP_END, A_LAST, attn)

            pe.wait_ge(s_sc, T)

            def total(k, r):
                wait(pe, r_cnt, ROUNDS * k + r + 1)
                wait(pe, r_j, ROUNDS * k + r)
                if r == 0:
                    wait(pe, r_slt, 2 * k)
                mm(bank[6][:, 0:TH + 1], ones_b[:, 0:P], cntb[:], True, True).then_inc(r_tot, 1)

            def ranks(k):
                wait(pe, r_ge, 2 * k + 2)
                wait(pe, r_j, ROUNDS * (k + 1 if searches(k) else k))
                wait(pe, r_slt, 2 * k)
                mm(bank[6][:, 32:32 + 2 * T], tri_b[:], GE[:], True, False)
                wait(pe, r_inc, k + 1)
                mm(bank[6][:, 32:32 + 2 * T], ones_b[:, 0:P], INC[:], False, True).then_inc(r_rank, 1)

            def tokens(k):
                wait(pe, r_htk, k + 1)
                wait(pe, r_loh, k + 1)
                wait(pe, r_Rxm, k)
                for t in range(T):
                    last = mm(bank[7][0:LO, 0:2 * LO], Loh[:, t, :], Htk[:, t].rearrange("p a h -> p (a h)"), t == 0, t == T - 1)
                last.then_inc(r_R, 1)

            def spread(k):
                wait(pe, r_Rt, k + 1)
                mm(bank[7][:, 32:32 + LO], expand, Rt[:, 0:LO], True, False)
                mm(bank[7][:, 32:32 + LO], expand, Rt[:, LO:], False, True).then_inc(r_Rx, 1)

            def rows(e, v, h):
                wait(pe, e_yT, 4 * e)
                for a in range(ST):
                    wait(pe, e_g[2 * v + a], 16 * h)
                    for c in range(CC):
                        last = nc.tensor.transpose(bank[0][:, c * CAP + a * P:c * CAP + (a + 1) * P],
                                                   G[:, v, a, c * P:(c + 1) * P], ident)
                last.then_inc(e_gT, 1)

            def up(e, v, f):
                if f == 0:
                    wait(pe, e_w1l, CC * (e + 1))
                g, q = f // 2, f % 2
                if q == 0:
                    if g == 3:
                        wait(pe, e_hs, FC * e + 2)
                    else:
                        wait(pe, e_hs, FC * (e - 1) + (8 if g == 0 else 2 * g + 2))
                for c in range(CC):
                    if f == 0:
                        wait(pe, e_yl, CC * e + c + 1)
                    last = mm3(bank[1 + g % 3][:, q * CAP:(q + 1) * CAP], lambda i: w1p[:, i, v, c, f * P:(f + 1) * P],
                               lambda i: yT[:, i, v, c, :], c == 0, c == CC - 1)
                if q == 1:
                    last.then_inc(e_h, 1)

            def down(e, v, n, h):
                a, f = n // FC, n % FC
                if n == 0:
                    wait(pe, e_w2[v], 16 * h)
                    wait(pe, e_fin, ST * (e - 1) + 1)
                if n == FC:
                    wait(pe, e_fin, ST * e)
                if a == 0:
                    wait(pe, e_hs, FC * e + f + 1)
                last = mm(bank[4 + a][:, 0:C], hT[:, v, f, a * P:(a + 1) * P], w2s[:, v, f, :], f == 0, f == FC - 1)
                if f == FC - 1:
                    last.then_inc(e_o, 1)

            UP = {0: (2, 4), 1: (4, 6), 2: (6, 7), 3: (7, 8)}
            DOWN = {1: (0, 1), 3: (1, 4), 4: (4, 7), 5: (7, 11), 6: (11, 13), 7: (13, 16)}

            def experts(k, u):
                if live(k - 2, E):
                    for f in range(0, 2):
                        up(k - 2, u, f)
                for r in range(ROUNDS):
                    if searches(k):
                        total(k, r)
                    if r == 2 and live(k - 1, E):
                        tokens(k - 1)
                    if r == 2 and live(k, E) and not searches(k):
                        ranks(k)
                    if r == 6 and live(k - 1, E):
                        rows(k - 1, 1 - u, (k + 1) // 2)
                    if live(k - 2, E):
                        for f in range(*UP.get(r, (0, 0))):
                            up(k - 2, u, f)
                        for n in range(*DOWN.get(r, (0, 0))):
                            down(k - 2, u, n, k // 2)
                    if r == 2 and live(k - 1, E):
                        spread(k - 1)
                if searches(k):
                    ranks(k)
            steps(pe, R_FIRST, R_LOOP, R_LOOP_END, R_LAST, experts)


_NAMES = ["x", "ctxT", "wqT", "wk", "wv", "wo", "wth1", "wth2T", "centT", "gb", "w1", "b1", "w2", "b2", "consts", "iconsts"]


def kernel(**inputs):
    import numpy as np
    import concourse.bacc as bacc
    from concourse import mybir as mb
    from concourse.bass_utils import run_bass_kernel_spmd as run

    a = {k: np.asarray(v) for k, v in inputs.items()}
    g, b = a["L0_ffn_ln_g"], a["L0_ffn_ln_b"]
    consts = np.zeros((P, C_END), np.float32)
    p = np.arange(P)
    consts[:, C_ID:C_ID + P] = p[:, None] == p
    consts[:, C_TRI:C_TRI + P] = (p[:, None] < p) - 1.0
    consts[:, C_I8:C_I8 + K8] = p[:, None] % K8 == np.arange(K8)
    consts[:, C_IOTA:C_IOTA + LO] = np.arange(LO)
    consts[:, C_TOK:C_TOK + 2 * T:2] = np.arange(T) * P
    consts[:, C_TOK + 1:C_TOK + 2 * T:2] = p[:, None]
    consts[:, C_SM:C_SM + LO] = np.arange(LO) % 8 == p[:, None] // LO
    for r in range(ROUNDS):
        w = consts[:, C_W + r * (TH + 1):C_W + (r + 1) * (TH + 1)]
        w[:, :TH] = 2.0 ** (32 - BITS * (r + 1))
        if r == DIRECT:
            w[:, TH // 2 + 1:TH] *= 2.0
        w[:, TH] = BASE if r >= DIRECT else 0.0
    consts[:, C_W + 7] *= -7.0
    consts[:LO, C_EX:C_EX + P] = np.arange(LO)[:, None] == p % LO
    ic = np.zeros((ROUNDS, TH), np.int64)
    for r in range(ROUNDS):
        ic[r] = np.arange(1, TH + 1) << (32 - BITS * (r + 1))
        if r > DIRECT and (r - DIRECT) % 2:
            ic[r] ^= BASE_BITS
    ic[0] = np.where(ic[0] >= 2 ** 31, ic[0] ^ 2 ** 31, ic[0] ^ (2 ** 32 - 1))
    ic = np.concatenate([ic.reshape(-1), [BASE_BITS if (ROUNDS - DIRECT) % 2 else 0]])
    iconsts = np.ascontiguousarray(np.broadcast_to(ic.reshape(1, -1), (P, ROUNDS * TH + 1))).astype(np.uint32).view(np.int32)
    arrays = {
        "x": a["x"].reshape(B * Q, C),
        "ctxT": a["ctx_1024"].reshape(B * K, C).T,
        "wqT": a["L0_xattn_Wq"].transpose(1, 2, 0).reshape(HD, C),
        "wk": a["L0_xattn_Wk"].reshape(C, HD),
        "wv": a["L0_xattn_Wv"].reshape(C, HD),
        "wo": a["L0_xattn_Wo"].reshape(HD, C),
        "wth1": a["L0_xattn_Wth1"],
        "wth2T": a["L0_xattn_Wth2"].T,
        "centT": a["L0_ffn_centroids"].T,
        "gb": np.stack([g.reshape(CC, P).T, b.reshape(CC, P).T], 1).reshape(P, 2 * CC),
        "w1": a["L0_ffn_w1"],
        "b1": a["L0_ffn_b1"].reshape(E * FC, P).T,
        "w2": a["L0_ffn_w2"],
        "b2": a["L0_ffn_b2"],
        "consts": consts,
        "iconsts": iconsts,
    }
    arrays = {k + "_dram": np.ascontiguousarray(v) for k, v in arrays.items()}
    nc = bacc.Bacc("TRN2", target_bir_lowering=False, num_devices=1)
    args = [nc.dram_tensor(n + "_dram", arrays[n + "_dram"].shape, mb.dt.from_np(arrays[n + "_dram"].dtype),
                           kind="ExternalInput").ap() for n in _NAMES]
    out = nc.dram_tensor("out_dram", (B * Q, C), mb.dt.float32, kind="ExternalOutput").ap()
    build(nc, *args, out)
    r = run(nc, [arrays], core_ids=[0])
    return r.results[0]["out_dram"].reshape(B, Q, C)
```
